# Optimizing a Trainium2 kernel written in Bass

```python
import numpy as np
import jax
import jax.numpy as jnp

def _softmax(x, axis=-1):
    return jax.nn.softmax(x, axis=axis)
def _gelu(x):
    return jax.nn.gelu(x, approximate=True)
def _silu(x):
    return jax.nn.silu(x)
def _sigmoid(x):
    return jax.nn.sigmoid(x)
def _layernorm(x, axis=-1, eps=1e-5):
    m = jnp.mean(x, axis=axis, keepdims=True)
    v = jnp.var(x, axis=axis, keepdims=True)
    return (x - m) / jnp.sqrt(v + eps)
def _scatter_add(tgt, idx, src, axis=0):
    return tgt.at[idx].add(src)
def _segment_sum(src, seg, n):
    return jax.ops.segment_sum(src, seg, n)

kernel_name = 'mk_conv_seq_d1_conv_nchw256_904744'

def setup_inputs(seed: int = 0):
    np.random.seed(seed)
    _w = jnp.asarray
    def _rec_inputs():
        import jax
        import jax.numpy as jnp
        _gk = jax.random.key(seed)
        x = -0.0005207 + 1.001 * jax.random.normal(jax.random.fold_in(_gk, 1), (8, 256, 32, 32), jnp.float32)
        return x
    x = _rec_inputs()
    def _L0_conv_setup():
        import jax, jax.numpy as jnp
        import numpy as np
        DIM = 256
        DT_RANK = 32
        D_STATE = 16
        DEPTH = 12
        B, H, W = (8, 32, 32)
        LN_EPS = 1e-05

        def _ssm(x, dbc_w, dtp_w, dtp_b, A_log, Dp):
            A = -jnp.exp(A_log)
            dbc = jnp.einsum('bld,ed->ble', x, dbc_w)
            delta, Bm, Cm = jnp.split(dbc, [DT_RANK, DT_RANK + D_STATE], axis=-1)
            delta = jax.nn.softplus(jnp.einsum('blr,dr->bld', delta, dtp_w) + dtp_b)
            dA = jnp.exp(delta[..., None] * A)
            dBu = delta[..., None] * Bm[:, :, None, :] * x[..., None]

            def step(h, inputs):
                dA_t, dBu_t, C_t = inputs
                h = dA_t * h + dBu_t
                y = jnp.einsum('bdn,bn->bd', h, C_t)
                return (h, y)
            h0 = jnp.zeros((x.shape[0], x.shape[2], D_STATE), x.dtype)
            _, ys = jax.lax.scan(step, h0, (dA.transpose(1, 0, 2, 3), dBu.transpose(1, 0, 2, 3), Cm.transpose(1, 0, 2)))
            y = ys.transpose(1, 0, 2)
            return y + x * Dp

        def _block(x, p):
            ln_g, ln_b, pw, pb, cfw, cfb, cbw, cbb, dbcw, dtpw, dtpb, alog, dp = p
            skip = x
            mu = x.mean(-1, keepdims=True)
            var = ((x - mu) ** 2).mean(-1, keepdims=True)
            xn = (x - mu) / jnp.sqrt(var + LN_EPS) * ln_g + ln_b
            xp = jnp.einsum('bld,ed->ble', xn, pw) + pb
            z = jax.nn.silu(xp)
            xf = jax.nn.softplus(jnp.einsum('bld,ed->ble', xp, cfw) + cfb)
            x1 = _ssm(xf, dbcw, dtpw, dtpb, alog, dp)
            xr = xp[:, ::-1, :]
            xb = jax.nn.softplus(jnp.einsum('bld,ed->ble', xr, cbw) + cbb)
            x2 = _ssm(xb, dbcw, dtpw, dtpb, alog, dp)[:, ::-1, :]
            return x1 * z + x2 * z + skip
        key = jax.random.key(seed)
        ks = jax.random.split(key, 8)
        d, r, n, L = (DIM, DT_RANK, D_STATE, DEPTH)

        def nrm(k, shape, scale=0.02):
            return jax.random.normal(k, shape, dtype=jnp.float32) * scale
        A_log = jnp.tile(jnp.log(jnp.arange(1, n + 1, dtype=jnp.float32))[None, None, :], (L, d, 1))
        return {'x': jax.random.normal(ks[0], (B, d, H, W), dtype=jnp.float32), 'ln_g': jnp.ones((L, d), jnp.float32), 'ln_b': jnp.zeros((L, d), jnp.float32), 'proj_w': nrm(ks[1], (L, d, d)), 'proj_b': jnp.zeros((L, d), jnp.float32), 'convf_w': nrm(ks[2], (L, d, d)), 'convf_b': jnp.zeros((L, d), jnp.float32), 'convb_w': nrm(ks[3], (L, d, d)), 'convb_b': jnp.zeros((L, d), jnp.float32), 'dbc_w': nrm(ks[4], (L, r + 2 * n, d)), 'dtp_w': nrm(ks[5], (L, d, r)), 'dtp_b': jnp.zeros((L, d), jnp.float32), 'A_log': A_log, 'D_param': jnp.ones((L, d), jnp.float32)}
    _L0_conv_all = _L0_conv_setup()
    _L0_conv_in = {k: v for k, v in _L0_conv_all.items() if k in ('ln_g', 'ln_b', 'proj_w', 'proj_b', 'convf_w', 'convf_b', 'convb_w', 'convb_b', 'dbc_w', 'dtp_w', 'dtp_b', 'A_log', 'D_param', )}
    del _L0_conv_all

    return {
        "x": x,
        "L0_conv_ln_g": _L0_conv_in["ln_g"],
        "L0_conv_ln_b": _L0_conv_in["ln_b"],
        "L0_conv_proj_w": _L0_conv_in["proj_w"],
        "L0_conv_proj_b": _L0_conv_in["proj_b"],
        "L0_conv_convf_w": _L0_conv_in["convf_w"],
        "L0_conv_convf_b": _L0_conv_in["convf_b"],
        "L0_conv_convb_w": _L0_conv_in["convb_w"],
        "L0_conv_convb_b": _L0_conv_in["convb_b"],
        "L0_conv_dbc_w": _L0_conv_in["dbc_w"],
        "L0_conv_dtp_w": _L0_conv_in["dtp_w"],
        "L0_conv_dtp_b": _L0_conv_in["dtp_b"],
        "L0_conv_A_log": _L0_conv_in["A_log"],
        "L0_conv_D_param": _L0_conv_in["D_param"],
    }

def reference(x, L0_conv_ln_g, L0_conv_ln_b, L0_conv_proj_w, L0_conv_proj_b, L0_conv_convf_w, L0_conv_convf_b, L0_conv_convb_w, L0_conv_convb_b, L0_conv_dbc_w, L0_conv_dtp_w, L0_conv_dtp_b, L0_conv_A_log, L0_conv_D_param):
    import jax
    import jax.numpy as jnp
    def _L0_conv_ref(x, ln_g, ln_b, proj_w, proj_b, convf_w, convf_b, convb_w, convb_b, dbc_w, dtp_w, dtp_b, A_log, D_param):
        import jax, jax.numpy as jnp
        import numpy as np
        DIM = 256
        DT_RANK = 32
        D_STATE = 16
        DEPTH = 12
        B, H, W = (8, 32, 32)
        LN_EPS = 1e-05

        def _ssm(x, dbc_w, dtp_w, dtp_b, A_log, Dp):
            A = -jnp.exp(A_log)
            dbc = jnp.einsum('bld,ed->ble', x, dbc_w)
            delta, Bm, Cm = jnp.split(dbc, [DT_RANK, DT_RANK + D_STATE], axis=-1)
            delta = jax.nn.softplus(jnp.einsum('blr,dr->bld', delta, dtp_w) + dtp_b)
            dA = jnp.exp(delta[..., None] * A)
            dBu = delta[..., None] * Bm[:, :, None, :] * x[..., None]

            def step(h, inputs):
                dA_t, dBu_t, C_t = inputs
                h = dA_t * h + dBu_t
                y = jnp.einsum('bdn,bn->bd', h, C_t)
                return (h, y)
            h0 = jnp.zeros((x.shape[0], x.shape[2], D_STATE), x.dtype)
            _, ys = jax.lax.scan(step, h0, (dA.transpose(1, 0, 2, 3), dBu.transpose(1, 0, 2, 3), Cm.transpose(1, 0, 2)))
            y = ys.transpose(1, 0, 2)
            return y + x * Dp

        def _block(x, p):
            ln_g, ln_b, pw, pb, cfw, cfb, cbw, cbb, dbcw, dtpw, dtpb, alog, dp = p
            skip = x
            mu = x.mean(-1, keepdims=True)
            var = ((x - mu) ** 2).mean(-1, keepdims=True)
            xn = (x - mu) / jnp.sqrt(var + LN_EPS) * ln_g + ln_b
            xp = jnp.einsum('bld,ed->ble', xn, pw) + pb
            z = jax.nn.silu(xp)
            xf = jax.nn.softplus(jnp.einsum('bld,ed->ble', xp, cfw) + cfb)
            x1 = _ssm(xf, dbcw, dtpw, dtpb, alog, dp)
            xr = xp[:, ::-1, :]
            xb = jax.nn.softplus(jnp.einsum('bld,ed->ble', xr, cbw) + cbb)
            x2 = _ssm(xb, dbcw, dtpw, dtpb, alog, dp)[:, ::-1, :]
            return x1 * z + x2 * z + skip
        b, c, h, w = x.shape
        seq = x.reshape(b, c, h * w).transpose(0, 2, 1)
        params = (ln_g, ln_b, proj_w, proj_b, convf_w, convf_b, convb_w, convb_b, dbc_w, dtp_w, dtp_b, A_log, D_param)

        def layer_step(s, p):
            return (_block(s, p), None)
        seq, _ = jax.lax.scan(layer_step, seq, params)
        return seq.transpose(0, 2, 1).reshape(b, c, h, w)

    def _gn(v, G=32, eps=1e-5):
        B_, C_, H_, W_ = v.shape
        g = v.reshape(B_, G, C_ // G, H_, W_)
        m = jnp.mean(g, axis=(2, 3, 4), keepdims=True)
        s = jnp.var(g, axis=(2, 3, 4), keepdims=True)
        return ((g - m) / jnp.sqrt(s + eps)).reshape(v.shape)

    def _ln_c(v, eps=1e-6):
        m = jnp.mean(v, axis=1, keepdims=True)
        s = jnp.var(v, axis=1, keepdims=True)
        return (v - m) / jnp.sqrt(s + eps)

    def _ln_t(v, eps=1e-5):
        m = jnp.mean(v, axis=-1, keepdims=True)
        s = jnp.var(v, axis=-1, keepdims=True)
        return (v - m) / jnp.sqrt(s + eps)

    def _to_tokens(v):
        B_, C_, H_, W_ = v.shape
        return v.reshape(B_, C_, H_ * W_).transpose(0, 2, 1)
    def _from_tokens(t, like):
        B_, C_, H_, W_ = like.shape
        return t.transpose(0, 2, 1).reshape(B_, C_, H_, W_)

    x = _L0_conv_ref(x, L0_conv_ln_g, L0_conv_ln_b, L0_conv_proj_w, L0_conv_proj_b, L0_conv_convf_w, L0_conv_convf_b, L0_conv_convb_w, L0_conv_convb_b, L0_conv_dbc_w, L0_conv_dtp_w, L0_conv_dtp_b, L0_conv_A_log, L0_conv_D_param)
    return x


_drawn_inputs = setup_inputs


def setup_inputs(seed=0):
    import zlib

    import numpy as np

    out = dict(_drawn_inputs(seed))
    spreads = {'L0_conv_ln_g': (1.0, 0.2),
     'L0_conv_ln_b': (0.0, 0.1),
     'L0_conv_proj_b': (0.0, 0.1),
     'L0_conv_convf_b': (0.0, 0.313),
     'L0_conv_convb_b': (0.0, 0.314),
     'L0_conv_dtp_b': (0.0, 0.8),
     'L0_conv_D_param': (1.0, 0.2)}
    factors = {'L0_conv_dtp_w': 25.951}
    for name, (base, spread) in spreads.items():
        noise = np.random.default_rng([zlib.crc32(name.encode()), seed]).standard_normal(out[name].shape)
        drawn = base * np.exp(spread * noise) if base else spread * noise
        out[name] = jnp.asarray(drawn.astype(out[name].dtype))
    for name, factor in factors.items():
        out[name] = (out[name] * factor).astype(out[name].dtype)
    return out
```

```python
from contextlib import ExitStack

import concourse.bass as bass
from concourse import mybir
from concourse.alu_op_type import AluOpType as ALU

ACT = mybir.ActivationFunctionType
F32 = mybir.dt.float32
BF16 = mybir.dt.bfloat16

P = 128
HALF = 512
EPS = 1e-5
TABLES = "natural_log_exp_and_others"


def conv_seq_kernel(nc, x, ln_g, ln_b, proj_w, proj_b, convf_w, convf_b, convb_w, convb_b,
                    dbc_w, dtp_w, dtp_b, A_log, D_param, out):
    LAYERS, D = ln_g.shape
    NB, _, HH, WW = x.shape
    T = HH * WW
    DT = D // P
    NH = T // HALF
    RANK = dtp_w.shape[2]
    NS = A_log.shape[2]
    BC = 2 * NS
    DIRS = 2
    GROUPS = DIRS * NS
    TILES = GROUPS * DT
    FILLS = DT * NH
    assert DT == 2 and NH == 2 and BC == 32 and RANK == 32 and NB % 2 == 0

    NDA, NV, NHB, NP, NC = 2, 2, 4, 2, 2
    SEED = 8
    LAG = 3
    N_VEC = 7
    G_, B_, PB_, CFB_, CBB_, DTB_, DP_ = range(N_VEC)
    RAW_DMAS = 3 + 4 + 1 + 1 + N_VEC

    x_d = x.rearrange("b (c p) h w -> b p c (h w)", p=P)
    out_d = out.rearrange("b (c p) h w -> b p c (h w)", p=P)

    with ExitStack() as ctx:
        def sb(name, shape, dt=F32):
            return ctx.enter_context(nc.sbuf_tensor(name, shape, dt))

        def sem(name):
            return ctx.enter_context(nc.semaphore(name))

        y = ctx.enter_context(nc.psum_tensor("y", [P, DT, T], F32))
        b_rep = ctx.enter_context(nc.psum_tensor("b_rep", [P, T], F32))
        c_rep = ctx.enter_context(nc.psum_tensor("c_rep", [P, HALF], F32))
        bank = ctx.enter_context(nc.psum_tensor("bank", [P, HALF], F32))

        xin = sb("xin", [P, DT, T])
        w = [sb(f"w{s}", [P, DT, T]) for s in range(2)]
        z = [sb(f"z{s}", [P, DT, T]) for s in range(2)]
        delta0 = sb("delta0", [P, DT, T])
        u0 = sb("u0", [P, DT, T])
        parts0 = sb("parts0", [P, T], BF16)
        delta1 = [sb(f"delta1_{s}", [P, DT, T]) for s in range(2)]
        u1 = [sb(f"u1_{s}", [P, DT, T]) for s in range(2)]
        parts1 = [sb(f"parts1_{s}", [P, T], BF16) for s in range(2)]
        a_step = [sb(f"a_step{s}", [P, DT, NS]) for s in range(2)]
        tmp = sb("tmp", [P, DT, T])
        xp = sb("xp", [P, DT, T])
        pre = sb("pre", [P, DT, T])
        xf = sb("xf", [P, DT, T])
        dbc = sb("dbc", [P, T])

        def delta_of(d, s):
            return delta1[s] if d else delta0

        def u_of(d, s):
            return u1[s] if d else u0

        def parts_of(d, s):
            return parts1[s] if d else parts0

        def xs_of(d, s):
            return w[s] if d else xf

        dA = [sb(f"dA{i}", [P, T]) for i in range(NDA)]
        v = [sb(f"v{i}", [P, T]) for i in range(NV)]
        hst = [sb(f"h{i}", [P, T]) for i in range(NHB)]
        prod = [sb(f"p{i}", [P, T]) for i in range(NP)]
        c_sb = [sb(f"c{i}", [P, T]) for i in range(NC)]

        raw_w = [sb(f"raw_w{i}", [P, DT, D]) for i in range(3)]
        raw_dbc = sb("raw_dbc", [P, D])
        raw_dtp = sb("raw_dtp", [P, DT, P])
        raw_vec = sb("raw_vec", [P, N_VEC, DT])
        raw_a = sb("raw_a", [P, DT, NS])
        wt = [sb(f"wt{i}", [P, DT, D]) for i in range(3)]
        wt_dbc = sb("wt_dbc", [P, 2 * DT, P])
        vec = sb("vec", [P, N_VEC, DT])
        pbias = sb("pbias", [P, DT])
        a_cur = sb("a_cur", [P, DT, NS])
        ident = sb("ident", [P, P])
        mean_w = sb("mean_w", [P, P])
        select = sb("select", [P, BC, P], BF16)
        eps = sb("eps", [P, 1])

        consts_clear = sem("consts_clear")
        consts_ready = sem("consts_ready")
        raw_loaded = sem("raw_loaded")
        vec_copied = sem("vec_copied")
        turned = sem("turned")
        turned_out = sem("turned_out")
        bias_sum = sem("bias_sum")
        bias_ready = sem("bias_ready")
        a_exp = sem("a_exp")
        a_neg = sem("a_neg")
        scaled = sem("scaled")

        x_loaded = sem("x_loaded")
        stored = sem("stored")
        mean_ready = sem("mean_ready")
        centred = sem("centred")
        squared = sem("squared")
        var_ready = sem("var_ready")
        logvar = sem("logvar")
        rstd_ready = sem("rstd_ready")
        normed = sem("normed")
        proj_ready = sem("proj_ready")
        xp_ready = sem("xp_ready")
        conv_ready = sem("conv_ready")
        conv_out = sem("conv_out")
        abs_done = sem("abs_done")
        exp_done = sem("exp_done")
        ln_done = sem("ln_done")
        gate_log = sem("gate_log")
        gate_sig = sem("gate_sig")
        gate_ready = sem("gate_ready")
        xs_ready = sem("xs_ready")
        dbc_ready = sem("dbc_ready")
        dbc_out = sem("dbc_out")
        dtp_ready = sem("dtp_ready")
        dtp_out = sem("dtp_out")
        hi_ready = sem("hi_ready")
        rest_ready = sem("rest_ready")
        mid_ready = sem("mid_ready")
        parts_ready = sem("parts_ready")
        delta_ready = sem("delta_ready")
        u_ready = sem("u_ready")
        xsum_ready = sem("xsum_ready")
        dxz_ready = sem("dxz_ready")
        w_ready = sem("w_ready")
        a_ready = sem("a_ready")
        gated = sem("gated")
        out_ready = sem("out_ready")

        da_ready = sem("da_ready")
        v_ready = sem("v_ready")
        h_ready = sem("h_ready")
        p_ready = sem("p_ready")
        summed = sem("summed")
        b_ready = sem("b_ready")
        c_filled = sem("c_filled")
        c_ready = sem("c_ready")

        def tiles(it, k):
            return it * TILES + (SEED + k)

        CHAINS = 5
        conv_chain = [1, 3]
        delta_chain = [2, 4]

        layers_steps = [(e, h) for h in range(NH) for e in range(DT)]

        def half(h):
            return slice(h * HALF, (h + 1) * HALF)

        block = ctx.enter_context(nc.Block())

        def run_layers(e, weights, step, prepare, load_raw=None):
            if load_raw:
                load_raw(0)
            weights(0, 0)
            for k in range(TILES):
                prepare(k, 0, 0)
            with e.Fori(0, LAYERS - 1) as layer:
                if load_raw:
                    load_raw(layer + 1)
                with e.Fori(0, NB // 2 - 1) as pair:
                    it = layer * NB + pair * 2
                    step(it, 0, True)
                    step(it + 1, 1, True)
                it = layer * NB + (NB - 2)
                step(it, 0, True)
                weights(layer + 1, it + 2)
                step(it + 1, 1, True)
            last = (LAYERS - 1) * NB
            with e.Fori(0, NB // 2 - 1) as pair:
                it = pair * 2 + last
                step(it, 0, True)
                step(it + 1, 1, True)
            step(last + NB - 2, 0, True)
            step(last + NB - 1, 1, False)

        @block.sync
        def _(sp):
            def load(src, added, b):
                sp.wait_ge(w_ready, added)
                sp.dma_start(xin[:], src[b]).then_inc(x_loaded, 16)

            def store(finished, s, b):
                sp.wait_ge(out_ready, finished)
                sp.dma_start(out_d[b], z[s][:]).then_inc(stored, 16)

            load(x_d, 0, 0)
            load(x_d, 1, 1)
            for it in range(NB - 2):
                load(x_d, it + 2, it + 2)
                store(it + 1, it % 2, it)
            with sp.Fori(0, (LAYERS - 1)) as layer:
                it0 = layer * NB + (NB - 2)
                for k in range(NB):
                    load(out_d, it0 + (k + 2), k)
                    store(it0 + (k + 1), k % 2, (NB - 2 + k) % NB)
            n = LAYERS * NB
            for it in (n - 2, n - 1):
                store(it + 1, it % 2, it % NB)
            sp.wait_ge(stored, 16 * n)

        @block.gpsimd
        def _(pool):
            nc.gpsimd.memset(ident[:], 0.0).then_inc(consts_clear, 1)
            nc.gpsimd.memset(select[:], 0.0).then_inc(consts_clear, 1)
            nc.gpsimd.memset(raw_dtp[:], 0.0).then_inc(consts_ready, 1)
            nc.gpsimd.memset(mean_w[:], 1.0 / D).then_inc(consts_ready, 1)
            nc.gpsimd.memset(eps[:], EPS).then_inc(consts_ready, 1)
            pool.wait_ge(consts_clear, 2)
            nc.gpsimd.affine_select(out=ident[:], in_=ident[:], compare_op=ALU.not_equal, fill=1.0,
                                    base=0, pattern=[[-1, P]], channel_multiplier=1).then_inc(consts_ready, 1)
            for part in range(3):
                pool.wait_ge(consts_clear, 2 + part)
                nc.gpsimd.affine_select(out=select[:], in_=select[:], compare_op=ALU.not_equal, fill=1.0,
                                        base=-BC * part, pattern=[[-1, BC], [0, P]],
                                        channel_multiplier=1).then_inc(consts_clear, 1)
            pool.wait_ge(consts_clear, 5)
            pool.sem_inc(consts_ready, 1)
            pool.sem_inc(p_ready, SEED)

            def weights(layer, n):
                pass

            def product(it, k, s):
                g = k // DT
                pool.wait_ge(h_ready, tiles(it, k + 1))
                pool.wait_ge(c_ready, it * (2 * GROUPS) + (2 * g + 2))
                pool.wait_ge(summed, tiles(it, k + 1 - NP))
                nc.gpsimd.tensor_tensor(prod[k % NP][:], hst[k % NHB][:], c_sb[g % NC][:],
                                        ALU.mult).then_inc(p_ready, 1)

            def prepare(k, n, s):
                for h in range(NH):
                    if k == 11 + 2 * h:
                        pool.wait_ge(rstd_ready, n * 2 + (h + 1))
                        pool.wait_ge(centred, n * 2 + (h + 1))
                        wh = w[s][:, :, half(h)]
                        nc.gpsimd.tensor_tensor(wh, wh, tmp[:, 0:1, half(h)].to_broadcast([P, DT, HALF]),
                                                ALU.mult).then_inc(normed, 1)
                if k == 22:
                    pool.wait_ge(gate_sig, n + 1)
                    if not (isinstance(n, int) and n < 2):
                        pool.wait_ge(stored, (n - 1) * 16)
                    nc.gpsimd.tensor_tensor(z[s][:], xp[:], tmp[:], ALU.mult).then_inc(gate_ready, 1)
                for d in range(DIRS):
                    ps = parts_of(d, s)
                    if k == (34, 52)[d]:
                        pool.wait_ge(hi_ready, n * 2 + (d + 1))
                        pool.wait_ge(xs_ready, n * 2 + (d + 1))
                        nc.gpsimd.tensor_tensor(tmp[:, 0, :], dbc[:], ps[:], ALU.subtract).then_inc(rest_ready, 1)
                    if k == (41, 59)[d]:
                        pool.wait_ge(delta_ready, n * 2 + (d + 1))
                        if d == 0 and not isinstance(n, int):
                            pool.wait_ge(v_ready, tiles(n - 1, TILES // 2))
                        nc.gpsimd.tensor_tensor(u_of(d, s)[:], delta_of(d, s)[:], xs_of(d, s)[:],
                                                ALU.mult).then_inc(u_ready, 1)
                if k == 60:
                    pool.wait_ge(u_ready, n * 2 + 2)
                    nc.gpsimd.tensor_tensor(w[s][:], w[s][:], xf[:], ALU.add).then_inc(xsum_ready, 1)
                if k == 63:
                    pool.wait_ge(dxz_ready, n * 2 + 2)
                    nc.gpsimd.tensor_tensor(w[s][:], w[s][:], xin[:], ALU.add).then_inc(w_ready, 1)

            def step(it, s, more):
                for k in range(TILES):
                    product(it, k, s)
                    if more:
                        prepare(k, it + 1, 1 - s)

            run_layers(pool, weights, step, prepare)

        @block.scalar
        def _(act):
            nc.scalar.preload_act_table_set(TABLES)
            act.sem_inc(da_ready, SEED)
            act.wait_ge(consts_ready, 5)

            def load_raw(layer):
                act.wait_ge(turned_out, layer * 4)
                act.wait_ge(vec_copied, layer)
                act.wait_ge(a_exp, layer)
                one = slice(layer, layer + 1) if isinstance(layer, int) else bass.ds(layer, 1)
                for i, wd in enumerate((proj_w, convf_w, convb_w)):
                    act.dma_start(raw_w[i][:], wd[one].rearrange("o (c p) d -> p (o c) d", p=P)).then_inc(raw_loaded, 16)
                rows = dbc_w[one].rearrange("o e d -> (o e) d")
                for part in range(3):
                    act.dma_start(raw_dbc[BC * part:BC * (part + 1), :], rows[RANK:RANK + BC, :]).then_inc(raw_loaded, 16)
                act.dma_start(raw_dbc[3 * BC:3 * BC + RANK, :], rows[0:RANK, :]).then_inc(raw_loaded, 16)
                act.dma_start(raw_dtp[:, :, P - RANK:P],
                              dtp_w[one].rearrange("o (c p) r -> p (o c) r", p=P)).then_inc(raw_loaded, 16)
                act.dma_start(raw_a[:], A_log[one].rearrange("o (c p) n -> p (o c) n", p=P)).then_inc(raw_loaded, 16)
                for i, vd in enumerate((ln_g, ln_b, proj_b, convf_b, convb_b, dtp_b, D_param)):
                    act.dma_start(raw_vec[:, i, :], vd[one].rearrange("o (c p) -> p (o c)", p=P),
                                  allow_slow_non_contiguous=True).then_inc(raw_loaded, 16)

            def weights(layer, n):
                act.wait_ge(raw_loaded, (layer + 1) * (16 * RAW_DMAS))
                act.wait_ge(a_ready, n)
                nc.scalar.activation(a_cur[:], raw_a[:], ACT.Exp).then_inc(a_exp, 1)
                for j in range(4):
                    act.wait_ge(turned, layer * 4 + (j + 1))
                    dst = wt[j][:].rearrange("p c d -> p (c d)") if j < 3 else wt_dbc[:].rearrange("p c d -> p (c d)")
                    nc.scalar.copy(dst, bank[:]).then_inc(turned_out, 1)

            def tile_exp(it, k, s):
                d, n, c = k // (NS * DT), (k // DT) % NS, k % DT
                if k == 0:
                    act.wait_ge(a_ready, it + 1)
                if k % (TILES // 2) == 0:
                    act.wait_ge(delta_ready, it * 2 + (d + 1))
                act.wait_ge(h_ready, tiles(it, k + 1 - NDA))
                nc.scalar.activation(dA[k % NDA][:], delta_of(d, s)[:, c, :], ACT.Exp,
                                     scale=a_step[s][:, c, n:n + 1]).then_inc(da_ready, 1)

            def copy_c(it, k):
                g, h = k // DT, k % DT
                act.wait_ge(c_filled, it * (2 * GROUPS) + (2 * g + h + 1))
                act.wait_ge(p_ready, tiles(it, DT * (g + 1 - NC)))
                nc.scalar.copy(c_sb[g % NC][:, half(h)], c_rep[:]).then_inc(c_ready, 1)

            def abs_exp(chain, n, src):
                nc.scalar.activation(tmp[:], src[:], ACT.Abs).then_inc(abs_done, 1)
                act.wait_ge(abs_done, n * CHAINS + (chain + 1))
                nc.scalar.activation(tmp[:], tmp[:], ACT.Exp, scale=-1.0).then_inc(exp_done, 1)

            def log1p(chain, n):
                act.wait_ge(exp_done, n * CHAINS + (chain + 1))
                nc.scalar.activation(tmp[:], tmp[:], ACT.Ln, bias=1.0).then_inc(ln_done, 1)

            def prepare(k, n, s):
                if k == 12:
                    rstd(n, 1)
                if k == 10:
                    rstd(n, 0)
                for h in range(NH):
                    if k == 8 + 2 * h:
                        act.wait_ge(centred, n * 2 + (h + 1))
                        act.wait_ge(delta_ready, n * 2)
                        nc.scalar.activation(pre[:, :, half(h)], w[s][:, :, half(h)], ACT.Square).then_inc(squared, 1)
                for i, (e, h) in enumerate(layers_steps):
                    if k == 13 + i:
                        act.wait_ge(proj_ready, n * FILLS + (i + 1))
                        act.wait_ge(bias_ready, 1)
                        nc.scalar.activation(xp[:, e, half(h)], bank[:], ACT.Identity,
                                             bias=pbias[:, e:e + 1]).then_inc(xp_ready, 1)
                if k == 17:
                    act.wait_ge(xp_ready, n * FILLS + FILLS)
                    act.wait_ge(normed, n * 2 + 2)
                    abs_exp(0, n, xp)
                if k == 18:
                    log1p(0, n)
                if k == 21:
                    act.wait_ge(gate_log, n + 1)
                    nc.scalar.activation(tmp[:], tmp[:], ACT.Exp).then_inc(gate_sig, 1)
                for d in range(DIRS):
                    for i, (e, h) in enumerate(layers_steps):
                        if k == (18, 41)[d] + i:
                            act.wait_ge(conv_ready, n * (2 * FILLS) + (d * FILLS + i + 1))
                            if d == 0:
                                act.wait_ge(var_ready, n * 2 + 2)
                            else:
                                act.wait_ge(delta_ready, n * 2 + 1)
                            nc.scalar.activation(pre[:, e, half(h)], bank[:], ACT.Identity,
                                                 bias=vec[:, CFB_ + d, e:e + 1]).then_inc(conv_out, 1)
                    if k == (24, 45)[d]:
                        act.wait_ge(conv_out, n * (2 * FILLS) + (d + 1) * FILLS)
                        if d == 0:
                            act.wait_ge(gate_ready, n + 1)
                        else:
                            act.wait_ge(delta_ready, n * 2 + 1)
                        abs_exp(conv_chain[d], n, pre)
                    if k == (25, 46)[d]:
                        log1p(conv_chain[d], n)
                    for h in range(NH):
                        if k == (29, 50)[d] + h:
                            act.wait_ge(dbc_ready, n * 4 + (2 * d + h + 1))
                            act.wait_ge(parts_ready, n * 2 + d)
                            nc.scalar.copy(dbc[:, half(h)], bank[:]).then_inc(dbc_out, 1)
                    for i, (e, h) in enumerate(layers_steps):
                        if k == (31, 52)[d] + i:
                            act.wait_ge(dtp_ready, n * (2 * FILLS) + (d * FILLS + i + 1))
                            act.wait_ge(xs_ready, n * 2 + (d + 1))
                            nc.scalar.activation(pre[:, e, half(h)], bank[:], ACT.Identity,
                                                 bias=vec[:, DTB_, e:e + 1]).then_inc(dtp_out, 1)
                    ps = parts_of(d, s)
                    if k == (33, 51)[d]:
                        act.wait_ge(dbc_out, n * 4 + (2 * d + 2))
                        nc.scalar.copy(ps[:], dbc[:]).then_inc(hi_ready, 1)
                    if k == (35, 53)[d]:
                        act.wait_ge(rest_ready, n * 2 + (d + 1))
                        for rows in (slice(BC, 2 * BC), slice(2 * BC, 3 * BC)):
                            nc.scalar.copy(ps[rows, :], tmp[rows, 0, :]).then_inc(mid_ready, 1)
                    if k == (38, 56)[d]:
                        act.wait_ge(dtp_out, n * (2 * FILLS) + (d + 1) * FILLS)
                        act.wait_ge(parts_ready, n * 2 + (d + 1))
                        abs_exp(delta_chain[d], n, pre)
                    if k == (39, 57)[d]:
                        log1p(delta_chain[d], n)

            def rstd(n, h):
                act.wait_ge(var_ready, n * 2 + (h + 1))
                act.wait_ge(delta_ready, n * 2)
                th = tmp[:, 0, half(h)]
                nc.scalar.activation(th, bank[:], ACT.Ln, bias=eps[:, 0:1]).then_inc(logvar, 1)
                act.wait_ge(logvar, n * 2 + (h + 1))
                nc.scalar.activation(th, th, ACT.Exp, scale=-0.5).then_inc(rstd_ready, 1)

            def step(it, s, more):
                for k in range(TILES):
                    tile_exp(it, k, s)
                    copy_c(it, k)
                    if more:
                        prepare(k, it + 1, 1 - s)

            run_layers(act, weights, step, prepare, load_raw)

        @block.tensor
        def _(pe):
            pe.sem_inc(summed, SEED)
            pe.wait_ge(consts_ready, 5)

            def weights(layer, n):
                pe.wait_ge(raw_loaded, (layer + 1) * (16 * RAW_DMAS))
                pe.wait_ge(dtp_out, n * (2 * FILLS))
                for j in range(4):
                    if j:
                        pe.wait_ge(turned_out, layer * 4 + j)
                    for q in range(4):
                        if j < 3:
                            src = raw_w[j][:, q % DT, (q // DT) * P:(q // DT + 1) * P]
                        else:
                            src = raw_dbc[:, q * P:(q + 1) * P] if q < DT else raw_dtp[:, q - DT, :]
                        mm = pe.transpose(bank[:, q * P:(q + 1) * P], src, ident[:])
                    mm.then_inc(turned, 1)
                pe.wait_ge(turned_out, layer * 4 + 4)
                pe.wait_ge(vec_copied, layer + 1)
                for e in range(DT):
                    for c in range(DT):
                        mm = pe.matmul(bank[:, e:e + 1], wt[0][:, c, e * P:(e + 1) * P],
                                       vec[:, B_, c:c + 1], start=(c == 0), stop=(c == DT - 1))
                mm.then_inc(bias_sum, 1)
                pe.wait_ge(scaled, (layer + 1) * DT)
                pe.wait_ge(bias_ready, layer + 1)

            def rep_b(it, g, s):
                d, n = g // NS, g % NS
                pe.wait_ge(parts_ready, it * 2 + (d + 1))
                pe.wait_ge(v_ready, tiles(it, DT * g))
                for h in range(NH):
                    mm = pe.matmul(b_rep[:, half(h)], select[:, n, :], parts_of(d, s)[:, half(h)],
                                   start=True, stop=True)
                mm.then_inc(b_ready, 1)

            def rep_c(it, k, s):
                g, h = k // DT, k % DT
                d, n = g // NS, g % NS
                pe.wait_ge(c_ready, it * (2 * GROUPS) + k)
                pe.matmul(c_rep[:], select[:, NS + n, :], parts_of(d, s)[:, half(h)],
                          start=True, stop=True).then_inc(c_filled, 1)

            def add_up(it, k):
                c = k % DT
                pe.wait_ge(p_ready, tiles(it, k + 1))
                if k == 0:
                    pe.wait_ge(gated, it)
                for h in range(NH):
                    mm = pe.matmul(y[:, c, half(h)], ident[:], prod[k % NP][:, half(h)],
                                   start=(k < DT), stop=(k >= TILES - DT), skip_group_check=True)
                mm.then_inc(summed, 1)

            def over_channels(lhs, rhs, h):
                for c in range(DT):
                    mm = pe.matmul(bank[:], lhs(c), rhs[:, c, half(h)], start=(c == 0), stop=(c == DT - 1))
                return mm

            def prepare(k, n, s):
                for h in range(NH):
                    if k == (3, 7)[h]:
                        pe.wait_ge(x_loaded, (n + 1) * 16)
                        if h == 0:
                            pe.wait_ge(dtp_out, n * (2 * FILLS))
                        else:
                            pe.wait_ge(centred, n * 2 + 1)
                        over_channels(lambda c: mean_w[:], xin, h).then_inc(mean_ready, 1)
                    if k == (9, 11)[h]:
                        pe.wait_ge(squared, n * 2 + (h + 1))
                        if h == 0:
                            pe.wait_ge(centred, n * 2 + 2)
                        else:
                            pe.wait_ge(logvar, n * 2 + 1)
                        over_channels(lambda c: mean_w[:], pre, h).then_inc(var_ready, 1)
                for i, (e, h) in enumerate(layers_steps):
                    cols = slice(e * P, (e + 1) * P)
                    if k == 12 + i:
                        pe.wait_ge(normed, n * 2 + (h + 1))
                        pe.wait_ge(xp_ready, n * FILLS + i)
                        if i == 0:
                            pe.wait_ge(logvar, n * 2 + 2)
                        over_channels(lambda c: wt[0][:, c, cols], w[s], h).then_inc(proj_ready, 1)
                    for d in range(DIRS):
                        if k == (17, 40)[d] + i:
                            pe.wait_ge(conv_out, n * (2 * FILLS) + (d * FILLS + i))
                            if i == 0 and d == 0:
                                pe.wait_ge(xp_ready, (n + 1) * FILLS)
                            if i == 0 and d == 1:
                                pe.wait_ge(dtp_out, n * (2 * FILLS) + FILLS)
                            over_channels(lambda c: wt[1 + d][:, c, cols], xp, h).then_inc(conv_ready, 1)
                        if k == (30, 51)[d] + i:
                            if i == 0:
                                pe.wait_ge(dbc_out, n * 4 + (2 * d + 2))
                            pe.wait_ge(dtp_out, n * (2 * FILLS) + (d * FILLS + i))
                            pe.matmul(bank[:], wt_dbc[:, DT + e, :], dbc[:, half(h)],
                                      start=True, stop=True).then_inc(dtp_ready, 1)
                for d in range(DIRS):
                    for h in range(NH):
                        if k == (28, 49)[d] + h:
                            pe.wait_ge(xs_ready, n * 2 + (d + 1))
                            if h == 0:
                                pe.wait_ge(conv_out, n * (2 * FILLS) + (d + 1) * FILLS)
                            else:
                                pe.wait_ge(dbc_out, n * 4 + (2 * d + 1))
                            over_channels(lambda c: wt_dbc[:, c, :], xs_of(d, s), h).then_inc(dbc_ready, 1)

            def step(it, s, more):
                if isinstance(it, int) and False:
                    pass
                for k in range(TILES):
                    if k % DT == 0:
                        if k == 0:
                            rep_b(it, 0, s)
                        if k // DT + 1 < GROUPS:
                            rep_b_next = k // DT + 1
                        else:
                            rep_b_next = None
                    rep_c(it, k, s)
                    if k % DT == 0 and rep_b_next is not None:
                        rep_b(it, rep_b_next, s)
                    if k >= LAG:
                        add_up(it, k - LAG)
                    if more:
                        prepare(k, it + 1, 1 - s)
                for k in range(TILES - LAG, TILES):
                    add_up(it, k)

            run_layers(pe, weights, step, prepare)

        @block.vector
        def _(dve):
            dve.sem_inc(v_ready, SEED)
            dve.sem_inc(h_ready, SEED)

            def weights(layer, n):
                dve.wait_ge(raw_loaded, (layer + 1) * (16 * RAW_DMAS))
                dve.wait_ge(delta_ready, n * 2)
                dve.wait_ge(dxz_ready, n * 2)
                nc.vector.tensor_copy(vec[:], raw_vec[:]).then_inc(vec_copied, 1)
                dve.wait_ge(a_exp, layer + 1)
                nc.vector.tensor_scalar(a_cur[:], a_cur[:], -1.0, None, ALU.mult).then_inc(a_neg, 1)
                dve.wait_ge(bias_sum, layer + 1)
                dve.wait_ge(vec_copied, layer + 1)
                nc.vector.tensor_tensor(pbias[:], bank[:, 0:DT], vec[:, PB_, :], ALU.add).then_inc(bias_ready, 1)
                for c in range(DT):
                    nc.vector.tensor_scalar(wt[0][:, c, :], wt[0][:, c, :], vec[:, G_, c:c + 1], None,
                                            ALU.mult).then_inc(scaled, 1)

            def times_b(it, k, s):
                d, c = k // (NS * DT), k % DT
                if k % (TILES // 2) == 0:
                    dve.wait_ge(u_ready, it * 2 + (d + 1))
                dve.wait_ge(b_ready, it * GROUPS + (k // DT + 1))
                dve.wait_ge(h_ready, tiles(it, k + 1 - NV))
                nc.vector.tensor_tensor(v[k % NV][:], u_of(d, s)[:, c, :], b_rep[:], ALU.mult).then_inc(v_ready, 1)

            def scan(it, k):
                d = k // (NS * DT)
                dve.wait_ge(v_ready, tiles(it, k + 1))
                dve.wait_ge(da_ready, tiles(it, k + 1))
                dve.wait_ge(p_ready, tiles(it, k + 1 - NHB))
                o, a, b = hst[k % NHB][:], dA[k % NDA][:], v[k % NV][:]
                if d:
                    o, a, b = o[:, ::-1], a[:, ::-1], b[:, ::-1]
                nc.vector.tensor_tensor_scan(o, a, b, 0.0, ALU.mult, ALU.add).then_inc(h_ready, 1)

            def finish(it, s):
                dve.wait_ge(summed, tiles(it, TILES))
                nc.vector.tensor_tensor(z[s][:], y[:], z[s][:], ALU.mult).then_inc(gated, 1)
                dve.wait_ge(gated, it + 1)
                dve.wait_ge(w_ready, it + 1)
                nc.vector.tensor_tensor(z[s][:], z[s][:], w[s][:], ALU.add).then_inc(out_ready, 1)

            def prepare(k, n, s):
                for h in range(NH):
                    if k == (6, 8)[h]:
                        dve.wait_ge(mean_ready, n * 2 + (h + 1))
                        if not isinstance(n, int):
                            dve.wait_ge(out_ready, n - 1)
                        nc.vector.tensor_tensor(w[s][:, :, half(h)], xin[:, :, half(h)],
                                                bank[:].unsqueeze(1).to_broadcast([P, DT, HALF]),
                                                ALU.subtract).then_inc(centred, 1)
                if k == 20:
                    dve.wait_ge(ln_done, n * CHAINS + 1)
                    nc.vector.scalar_tensor_tensor(tmp[:], xp[:], 0.0, tmp[:], ALU.min,
                                                   ALU.subtract).then_inc(gate_log, 1)
                for d in range(DIRS):
                    if k == (26, 48)[d]:
                        dve.wait_ge(ln_done, n * CHAINS + (conv_chain[d] + 1))
                        dve.wait_ge(u_ready, n * 2 + d)
                        dve.wait_ge(xsum_ready, n)
                        nc.vector.scalar_tensor_tensor(xs_of(d, s)[:], pre[:], 0.0, tmp[:], ALU.max,
                                                       ALU.add).then_inc(xs_ready, 1)
                    if k == (40, 58)[d]:
                        dve.wait_ge(ln_done, n * CHAINS + (delta_chain[d] + 1))
                        nc.vector.scalar_tensor_tensor(delta_of(d, s)[:], pre[:], 0.0, tmp[:], ALU.max,
                                                       ALU.add).then_inc(delta_ready, 1)
                for d in range(DIRS):
                    if k == (36, 54)[d]:
                        dve.wait_ge(mid_ready, n * 4 + (2 * d + 2))
                        ps, rows = parts_of(d, s), slice(2 * BC, 3 * BC)
                        nc.vector.tensor_tensor(ps[rows, :], tmp[rows, 0, :], ps[rows, :],
                                                ALU.subtract).then_inc(parts_ready, 1)
                if k == 56:
                    nc.vector.tensor_copy(a_step[s][:], a_cur[:]).then_inc(a_ready, 1)
                if k == 63:
                    dve.wait_ge(xsum_ready, n + 1)
                    dve.wait_ge(gate_ready, n + 1)
                    for c in range(DT):
                        nc.vector.scalar_tensor_tensor(w[s][:, c, :], w[s][:, c, :], vec[:, DP_, c:c + 1],
                                                       z[s][:, c, :], ALU.mult, ALU.mult).then_inc(dxz_ready, 1)

            def step(it, s, more):
                for g in range(GROUPS):
                    for c in range(DT):
                        times_b(it, g * DT + c, s)
                    for c in range(DT):
                        scan(it, g * DT + c)
                    if more:
                        for c in range(DT):
                            prepare(g * DT + c, it + 1, 1 - s)
                finish(it, s)

            run_layers(dve, weights, step, prepare)


_INS = ['x'] + ['L0_conv_' + n for n in ('ln_g', 'ln_b', 'proj_w', 'proj_b', 'convf_w', 'convf_b', 'convb_w',
                                         'convb_b', 'dbc_w', 'dtp_w', 'dtp_b', 'A_log', 'D_param')]
_OUTS = [((8, 256, 32, 32), 'float32')]


def kernel(**inputs):
    import numpy as _np
    import concourse.bacc as _bacc
    from concourse import mybir as _mybir
    from concourse.bass_utils import run_bass_kernel_spmd as _run

    nc = _bacc.Bacc("TRN2", target_bir_lowering=False, num_devices=1)
    arrays, args = {}, []
    for name in _INS:
        a = _np.ascontiguousarray(inputs[name])
        arrays[f"in_{name}_dram"] = a
        args.append(nc.dram_tensor(f"in_{name}_dram", a.shape, _mybir.dt.from_np(a.dtype), kind="ExternalInput").ap())
    for i, (shape, dtype) in enumerate(_OUTS):
        dt = _mybir.dt.from_np(_np.dtype(dtype))
        args.append(nc.dram_tensor(f"out_{i}_dram", shape, dt, kind="ExternalOutput").ap())
    conv_seq_kernel(nc, *args)
    r = _run(nc, [arrays], core_ids=[0])
    got = tuple(r.results[0][f"out_{i}_dram"] for i in range(len(_OUTS)))
    return got[0]
```

```python
from contextlib import ExitStack

import concourse.bass as bass
from concourse import mybir
from concourse.alu_op_type import AluOpType as ALU

ACT = mybir.ActivationFunctionType
F32 = mybir.dt.float32
BF16 = mybir.dt.bfloat16

P = 128
HALF = 512
EPS = 1e-5
TABLES = "natural_log_exp_and_others"


def conv_seq_kernel(nc, x, ln_g, ln_b, proj_w, proj_b, convf_w, convf_b, convb_w, convb_b,
                    dbc_w, dtp_w, dtp_b, A_log, D_param, out):
    LAYERS, D = ln_g.shape
    NB, _, HH, WW = x.shape
    T = HH * WW
    DT = D // P
    NH = T // HALF
    RANK = dtp_w.shape[2]
    NS = A_log.shape[2]
    BC = 2 * NS
    DIRS = 2
    GROUPS = DIRS * NS
    TILES = GROUPS * DT
    FILLS = DT * NH
    assert DT == 2 and NH == 2 and BC == 32 and RANK == 32 and NB % 2 == 0

    NDA, NR, NC = 2, 8, 4
    SEED = 8
    LAG0, LAG_LEAST, LAG_MOST = 4, 3, 5
    FIRST = 6
    FINISH = 2
    C_LEAD = 3
    AHEAD = 2
    N_VEC = 7
    G_, B_, PB_, CFB_, CBB_, DTB_, DP_ = range(N_VEC)
    RAW_DMAS = 4 + 1 + 1 + N_VEC

    x_d = x.rearrange("b (c p) h w -> b p c (h w)", p=P)
    out_d = out.rearrange("b (c p) h w -> b p c (h w)", p=P)

    with ExitStack() as ctx:
        def sb(name, shape, dt=F32):
            return ctx.enter_context(nc.sbuf_tensor(name, shape, dt))

        def sem(name):
            return ctx.enter_context(nc.semaphore(name))

        y = ctx.enter_context(nc.psum_tensor("y", [P, DT, T], F32))
        b_rep = ctx.enter_context(nc.psum_tensor("b_rep", [P, T], F32))
        c_rep = ctx.enter_context(nc.psum_tensor("c_rep", [P, HALF], F32))
        bank = ctx.enter_context(nc.psum_tensor("bank", [P, HALF], F32))

        xin = sb("xin", [P, DT, T])
        w = [sb(f"w{s}", [P, DT, T]) for s in range(2)]
        z = [sb(f"z{s}", [P, DT, T]) for s in range(2)]
        delta0 = sb("delta0", [P, DT, T])
        u0 = sb("u0", [P, DT, T])
        parts0 = sb("parts0", [P, T], BF16)
        delta1 = [sb(f"delta1_{s}", [P, DT, T]) for s in range(2)]
        u1 = [sb(f"u1_{s}", [P, DT, T]) for s in range(2)]
        parts1 = [sb(f"parts1_{s}", [P, T], BF16) for s in range(2)]
        a_step = [sb(f"a_step{s}", [P, DT, NS]) for s in range(2)]
        tmp = sb("tmp", [P, DT, T])
        xp = sb("xp", [P, DT, T])
        pre = sb("pre", [P, DT, T])
        xf = sb("xf", [P, DT, T])
        dbc = sb("dbc", [P, T])

        def delta_of(d, s):
            return delta1[s] if d else delta0

        def u_of(d, s):
            return u1[s] if d else u0

        def parts_of(d, s):
            return parts1[s] if d else parts0

        def xs_of(d, s):
            return w[s] if d else xf

        dA = [sb(f"dA{i}", [P, T]) for i in range(NDA)]
        ring = [sb(f"ring{i}", [P, T]) for i in range(NR)]
        c_sb = [sb(f"c{i}", [P, T]) for i in range(NC)]

        raw_w = sb("raw_w", [P, DT, D])
        raw_dbc = sb("raw_dbc", [P, D])
        raw_dtp = sb("raw_dtp", [P, DT, P])
        raw_vec = sb("raw_vec", [P, N_VEC, DT])
        raw_a = sb("raw_a", [P, DT, NS])
        wt = [sb(f"wt{i}", [P, DT, D]) for i in range(3)]
        wt_dbc = sb("wt_dbc", [P, 2 * DT, P])
        vec = sb("vec", [P, N_VEC, DT])
        pbias = sb("pbias", [P, DT])
        a_cur = sb("a_cur", [P, DT, NS])
        ident = sb("ident", [P, P])
        mean_w = sb("mean_w", [P, P])
        select = sb("select", [P, BC, P], BF16)
        eps = sb("eps", [P, 1])

        consts_clear = sem("consts_clear")
        consts_ready = sem("consts_ready")
        raw_loaded = sem("raw_loaded")
        square_loaded = sem("square_loaded")
        vec_copied = sem("vec_copied")
        turned = sem("turned")
        turned_out = sem("turned_out")
        bias_sum = sem("bias_sum")
        bias_ready = sem("bias_ready")
        a_exp = sem("a_exp")
        a_neg = sem("a_neg")
        scaled = sem("scaled")

        x_loaded = sem("x_loaded")
        stored = sem("stored")
        mean_ready = sem("mean_ready")
        centred = sem("centred")
        squared = sem("squared")
        var_ready = sem("var_ready")
        logvar = sem("logvar")
        rstd_ready = sem("rstd_ready")
        normed = sem("normed")
        proj_ready = sem("proj_ready")
        xp_ready = sem("xp_ready")
        conv_ready = sem("conv_ready")
        conv_out = sem("conv_out")
        abs_done = sem("abs_done")
        exp_done = sem("exp_done")
        ln_done = sem("ln_done")
        gate_log = sem("gate_log")
        gate_sig = sem("gate_sig")
        gate_ready = sem("gate_ready")
        xs_ready = sem("xs_ready")
        dbc_ready = sem("dbc_ready")
        dbc_out = sem("dbc_out")
        dtp_ready = sem("dtp_ready")
        dtp_out = sem("dtp_out")
        hi_ready = sem("hi_ready")
        rest_ready = sem("rest_ready")
        mid_ready = sem("mid_ready")
        parts_ready = sem("parts_ready")
        delta_ready = sem("delta_ready")
        u_ready = sem("u_ready")
        xsum_ready = sem("xsum_ready")
        dxz_ready = sem("dxz_ready")
        w_ready = sem("w_ready")
        a_ready = sem("a_ready")
        gated = sem("gated")
        out_ready = sem("out_ready")

        da_ready = sem("da_ready")
        v_ready = sem("v_ready")
        h_ready = sem("h_ready")
        p_ready = sem("p_ready")
        summed = sem("summed")
        b_ready = sem("b_ready")
        c_filled = sem("c_filled")
        c_ready = sem("c_ready")

        def tiles(it, k):
            return it * TILES + (SEED + k)

        CHAINS = 5
        conv_chain = [1, 3]
        delta_chain = [2, 4]

        layers_steps = [(e, h) for h in range(NH) for e in range(DT)]

        def half(h):
            return slice(h * HALF, (h + 1) * HALF)

        block = ctx.enter_context(nc.Block())

        def run_layers(weights, slots, prepare, begin, tail, load_raw, e, first=FIRST):
            def turn(it, s, more):
                slots(it, s, first, TILES, more > 0)
                if more:
                    slots(it + 1, 1 - s, 0, first, more > 1)
                else:
                    tail(it, s)

            load_raw(0)
            weights(0, 0)
            for k in range(TILES):
                prepare(k, 0, 0)
            begin()
            slots(0, 0, 0, first, True)
            with e.Fori(0, LAYERS - 1) as layer:
                load_raw(layer + 1)
                with e.Fori(0, NB // 2 - 1) as pair:
                    it = layer * NB + pair * 2
                    turn(it, 0, 2)
                    turn(it + 1, 1, 2)
                it = layer * NB + (NB - 2)
                turn(it, 0, 2)
                weights(layer + 1, it + 2)
                turn(it + 1, 1, 2)
            last = (LAYERS - 1) * NB
            with e.Fori(0, NB // 2 - 1) as pair:
                it = pair * 2 + last
                turn(it, 0, 2)
                turn(it + 1, 1, 2)
            turn(last + NB - 2, 0, 1)
            turn(last + NB - 1, 1, 0)

        def nothing(*_):
            pass

        @block.sync
        def _(sp):
            def load(src, added, b):
                sp.wait_ge(w_ready, added)
                sp.dma_start(xin[:], src[b]).then_inc(x_loaded, 16)

            def store(finished, s, b):
                sp.wait_ge(out_ready, finished)
                sp.dma_start(out_d[b], z[s][:]).then_inc(stored, 16)

            load(x_d, 0, 0)
            load(x_d, 1, 1)
            for it in range(NB - 2):
                load(x_d, it + 2, it + 2)
                store(it + 1, it % 2, it)
            with sp.Fori(0, (LAYERS - 1)) as layer:
                it0 = layer * NB + (NB - 2)
                for k in range(NB):
                    load(out_d, it0 + (k + 2), k)
                    store(it0 + (k + 1), k % 2, (NB - 2 + k) % NB)
            n = LAYERS * NB
            for it in (n - 2, n - 1):
                store(it + 1, it % 2, it % NB)
            sp.wait_ge(stored, 16 * n)

        @block.gpsimd
        def _(pool):
            nc.gpsimd.memset(ident[:], 0.0).then_inc(consts_clear, 1)
            nc.gpsimd.memset(select[:], 0.0).then_inc(consts_clear, 1)
            nc.gpsimd.memset(raw_dtp[:], 0.0).then_inc(consts_ready, 1)
            nc.gpsimd.memset(mean_w[:], 1.0 / D).then_inc(consts_ready, 1)
            nc.gpsimd.memset(eps[:], EPS).then_inc(consts_ready, 1)
            pool.wait_ge(consts_clear, 2)
            nc.gpsimd.affine_select(out=ident[:], in_=ident[:], compare_op=ALU.not_equal, fill=1.0,
                                    base=0, pattern=[[-1, P]], channel_multiplier=1).then_inc(consts_ready, 1)
            for part in range(3):
                pool.wait_ge(consts_clear, 2 + part)
                nc.gpsimd.affine_select(out=select[:], in_=select[:], compare_op=ALU.not_equal, fill=1.0,
                                        base=-BC * part, pattern=[[-1, BC], [0, P]],
                                        channel_multiplier=1).then_inc(consts_clear, 1)
            pool.wait_ge(consts_clear, 5)
            pool.sem_inc(consts_ready, 1)
            pool.sem_inc(p_ready, SEED)

            def product(it, k, s):
                g = k // DT
                pool.wait_ge(h_ready, tiles(it, k + 1))
                pool.wait_ge(c_ready, it * (2 * GROUPS) + (2 * g + 2))
                nc.gpsimd.tensor_tensor(ring[k % NR][:], ring[k % NR][:], c_sb[g % NC][:],
                                        ALU.mult).then_inc(p_ready, 1)

            def prepare(k, n, s):
                for h in range(NH):
                    if k == 13 + 2 * h:
                        pool.wait_ge(rstd_ready, n * 2 + (h + 1))
                        pool.wait_ge(centred, n * 2 + (h + 1))
                        wh = w[s][:, :, half(h)]
                        nc.gpsimd.tensor_tensor(wh, wh, tmp[:, 0:1, half(h)].to_broadcast([P, DT, HALF]),
                                                ALU.mult).then_inc(normed, 1)
                if k == 24:
                    pool.wait_ge(gate_sig, n + 1)
                    if not (isinstance(n, int) and n < 2):
                        pool.wait_ge(stored, (n - 1) * 16)
                    nc.gpsimd.tensor_tensor(z[s][:], xp[:], tmp[:], ALU.mult).then_inc(gate_ready, 1)
                for d in range(DIRS):
                    ps = parts_of(d, s)
                    if k == (34, 55)[d]:
                        pool.wait_ge(hi_ready, n * 2 + (d + 1))
                        pool.wait_ge(xs_ready, n * 2 + (d + 1))
                        nc.gpsimd.tensor_tensor(tmp[:, 0, :], dbc[:], ps[:], ALU.subtract).then_inc(rest_ready, 1)
                    if k == (43, 62)[d]:
                        pool.wait_ge(delta_ready, n * 2 + (d + 1))
                        if d == 0 and not isinstance(n, int):
                            pool.wait_ge(v_ready, tiles(n - 1, TILES // 2))
                        nc.gpsimd.tensor_tensor(u_of(d, s)[:], delta_of(d, s)[:], xs_of(d, s)[:],
                                                ALU.mult).then_inc(u_ready, 1)
                if k == 52:
                    pool.wait_ge(xs_ready, n * 2 + 2)
                    nc.gpsimd.tensor_tensor(xf[:], xf[:], w[s][:], ALU.add).then_inc(xsum_ready, 1)
                if k == 63:
                    pool.wait_ge(dxz_ready, n * 2 + 2)
                    pool.wait_ge(u_ready, n * 2 + 2)
                    nc.gpsimd.tensor_tensor(w[s][:], xf[:], xin[:], ALU.add).then_inc(w_ready, 1)

            def slots(it, s, k0, k1, more):
                for k in range(k0, k1):
                    product(it, k, s)
                    if more:
                        prepare(k, it + 1, 1 - s)

            run_layers(nothing, slots, prepare, nothing, nothing, nothing, pool)

        @block.scalar
        def _(act):
            nc.scalar.preload_act_table_set(TABLES)
            act.sem_inc(da_ready, SEED)
            act.wait_ge(consts_ready, 5)

            def load_square(j, one):
                wd = (proj_w, convf_w, convb_w)[j]
                act.dma_start(raw_w[:], wd[one].rearrange("o (c p) d -> p (o c) d", p=P)).then_inc(square_loaded, 16)

            def load_raw(layer):
                act.wait_ge(turned_out, layer * 4)
                act.wait_ge(vec_copied, layer)
                act.wait_ge(a_exp, layer)
                one = slice(layer, layer + 1) if isinstance(layer, int) else bass.ds(layer, 1)
                load_square(0, one)
                rows = dbc_w[one].rearrange("o e d -> (o e) d")
                for part in range(3):
                    act.dma_start(raw_dbc[BC * part:BC * (part + 1), :], rows[RANK:RANK + BC, :]).then_inc(raw_loaded, 16)
                act.dma_start(raw_dbc[3 * BC:3 * BC + RANK, :], rows[0:RANK, :]).then_inc(raw_loaded, 16)
                act.dma_start(raw_dtp[:, :, P - RANK:P],
                              dtp_w[one].rearrange("o (c p) r -> p (o c) r", p=P)).then_inc(raw_loaded, 16)
                act.dma_start(raw_a[:], A_log[one].rearrange("o (c p) n -> p (o c) n", p=P)).then_inc(raw_loaded, 16)
                for i, vd in enumerate((ln_g, ln_b, proj_b, convf_b, convb_b, dtp_b, D_param)):
                    act.dma_start(raw_vec[:, i, :], vd[one].rearrange("o (c p) -> p (o c)", p=P),
                                  allow_slow_non_contiguous=True).then_inc(raw_loaded, 16)

            def weights(layer, n):
                act.wait_ge(raw_loaded, (layer + 1) * (16 * RAW_DMAS))
                act.wait_ge(a_ready, n)
                nc.scalar.activation(a_cur[:], raw_a[:], ACT.Exp).then_inc(a_exp, 1)
                one = slice(layer, layer + 1) if isinstance(layer, int) else bass.ds(layer, 1)
                for j in range(4):
                    act.wait_ge(turned, layer * 4 + (j + 1))
                    if j < 2:
                        load_square(j + 1, one)
                    dst = wt[j][:].rearrange("p c d -> p (c d)") if j < 3 else wt_dbc[:].rearrange("p c d -> p (c d)")
                    nc.scalar.copy(dst, bank[:]).then_inc(turned_out, 1)
                act.wait_ge(vec_copied, layer + 1)
                act.wait_ge(bias_ready, layer + 1)

            def tile_exp(it, k, s):
                d, n, c = k // (NS * DT), (k // DT) % NS, k % DT
                if k == 0:
                    act.wait_ge(a_ready, it + 1)
                if k % (TILES // 2) == 0:
                    act.wait_ge(delta_ready, it * 2 + (d + 1))
                act.wait_ge(h_ready, tiles(it, k + 1 - NDA))
                nc.scalar.activation(dA[k % NDA][:], delta_of(d, s)[:, c, :], ACT.Exp,
                                     scale=a_step[s][:, c, n:n + 1]).then_inc(da_ready, 1)

            def copy_c(it, k):
                g, h = k // DT, k % DT
                act.wait_ge(c_filled, it * (2 * GROUPS) + (2 * g + h + 1))
                act.wait_ge(p_ready, tiles(it, DT * (g + 1 - NC)))
                nc.scalar.copy(c_sb[g % NC][:, half(h)], c_rep[:]).then_inc(c_ready, 1)

            def abs_exp(chain, n, src):
                nc.scalar.activation(tmp[:], src[:], ACT.Abs).then_inc(abs_done, 1)
                act.wait_ge(abs_done, n * CHAINS + (chain + 1))
                nc.scalar.activation(tmp[:], tmp[:], ACT.Exp, scale=-1.0).then_inc(exp_done, 1)

            def log1p(chain, n):
                act.wait_ge(exp_done, n * CHAINS + (chain + 1))
                nc.scalar.activation(tmp[:], tmp[:], ACT.Ln, bias=1.0).then_inc(ln_done, 1)

            def prepare(k, n, s):
                if k in (12, 14):
                    rstd(n, (k - 12) // 2)
                for h in range(NH):
                    if k == 10 + 2 * h:
                        act.wait_ge(centred, n * 2 + (h + 1))
                        act.wait_ge(delta_ready, n * 2)
                        nc.scalar.activation(pre[:, :, half(h)], w[s][:, :, half(h)], ACT.Square).then_inc(squared, 1)
                for i, (e, h) in enumerate(layers_steps):
                    if k == 15 + i:
                        act.wait_ge(proj_ready, n * FILLS + (i + 1))
                        nc.scalar.activation(xp[:, e, half(h)], bank[:], ACT.Identity,
                                             bias=pbias[:, e:e + 1]).then_inc(xp_ready, 1)
                if k == 19:
                    act.wait_ge(xp_ready, n * FILLS + FILLS)
                    act.wait_ge(normed, n * 2 + 2)
                    abs_exp(0, n, xp)
                if k == 20:
                    log1p(0, n)
                if k == 23:
                    act.wait_ge(gate_log, n + 1)
                    nc.scalar.activation(tmp[:], tmp[:], ACT.Exp).then_inc(gate_sig, 1)
                for d in range(DIRS):
                    for i, (e, h) in enumerate(layers_steps):
                        if k == (20, 44)[d] + i:
                            act.wait_ge(conv_ready, n * (2 * FILLS) + (d * FILLS + i + 1))
                            if d == 0:
                                act.wait_ge(var_ready, n * 2 + 2)
                            else:
                                act.wait_ge(delta_ready, n * 2 + 1)
                            nc.scalar.activation(pre[:, e, half(h)], bank[:], ACT.Identity,
                                                 bias=vec[:, CFB_ + d, e:e + 1]).then_inc(conv_out, 1)
                    if k == (26, 48)[d]:
                        act.wait_ge(conv_out, n * (2 * FILLS) + (d + 1) * FILLS)
                        if d == 0:
                            act.wait_ge(gate_ready, n + 1)
                        else:
                            act.wait_ge(delta_ready, n * 2 + 1)
                        abs_exp(conv_chain[d], n, pre)
                    if k == (27, 49)[d]:
                        log1p(conv_chain[d], n)
                    for h in range(NH):
                        if k == (30, 52)[d] + h:
                            act.wait_ge(dbc_ready, n * 4 + (2 * d + h + 1))
                            act.wait_ge(parts_ready, n * 2 + d)
                            nc.scalar.copy(dbc[:, half(h)], bank[:]).then_inc(dbc_out, 1)
                    for i, (e, h) in enumerate(layers_steps):
                        if k == (32, 54)[d] + i:
                            act.wait_ge(dtp_ready, n * (2 * FILLS) + (d * FILLS + i + 1))
                            act.wait_ge(xs_ready, n * 2 + (d + 1))
                            nc.scalar.activation(pre[:, e, half(h)], bank[:], ACT.Identity,
                                                 bias=vec[:, DTB_, e:e + 1]).then_inc(dtp_out, 1)
                    ps = parts_of(d, s)
                    if k == (33, 54)[d]:
                        act.wait_ge(dbc_out, n * 4 + (2 * d + 2))
                        nc.scalar.copy(ps[:], dbc[:]).then_inc(hi_ready, 1)
                    if k == (36, 57)[d]:
                        act.wait_ge(rest_ready, n * 2 + (d + 1))
                        for rows in (slice(BC, 2 * BC), slice(2 * BC, 3 * BC)):
                            nc.scalar.copy(ps[rows, :], tmp[rows, 0, :]).then_inc(mid_ready, 1)
                    if k == (39, 59)[d]:
                        act.wait_ge(dtp_out, n * (2 * FILLS) + (d + 1) * FILLS)
                        act.wait_ge(parts_ready, n * 2 + (d + 1))
                        abs_exp(delta_chain[d], n, pre)
                    if k == (40, 60)[d]:
                        log1p(delta_chain[d], n)

            def rstd(n, h):
                act.wait_ge(var_ready, n * 2 + (h + 1))
                act.wait_ge(delta_ready, n * 2)
                th = tmp[:, 0, half(h)]
                nc.scalar.activation(th, bank[:], ACT.Ln, bias=eps[:, 0:1]).then_inc(logvar, 1)
                act.wait_ge(logvar, n * 2 + (h + 1))
                nc.scalar.activation(th, th, ACT.Exp, scale=-0.5).then_inc(rstd_ready, 1)

            def slots(it, s, k0, k1, more):
                for k in range(k0, k1):
                    copy_c(it, k)
                    tile_exp(it, k, s)
                    if more:
                        prepare(k - AHEAD, it + 1, 1 - s)

            run_layers(weights, slots, prepare, nothing, nothing, load_raw, act, FIRST + AHEAD)

        @block.tensor
        def _(pe):
            pe.sem_inc(summed, SEED)
            pe.wait_ge(consts_ready, 5)

            def weights(layer, n):
                pe.wait_ge(raw_loaded, (layer + 1) * (16 * RAW_DMAS))
                pe.wait_ge(dtp_out, n * (2 * FILLS))
                for j in range(4):
                    if j < 3:
                        pe.wait_ge(square_loaded, layer * 48 + (16 * j + 16))
                    if j:
                        pe.wait_ge(turned_out, layer * 4 + j)
                    for q in range(4):
                        if j < 3:
                            src = raw_w[:, q % DT, (q // DT) * P:(q // DT + 1) * P]
                        else:
                            src = raw_dbc[:, q * P:(q + 1) * P] if q < DT else raw_dtp[:, q - DT, :]
                        mm = pe.transpose(bank[:, q * P:(q + 1) * P], src, ident[:])
                    mm.then_inc(turned, 1)
                pe.wait_ge(turned_out, layer * 4 + 4)
                pe.wait_ge(vec_copied, layer + 1)
                for e in range(DT):
                    for c in range(DT):
                        mm = pe.matmul(bank[:, e:e + 1], wt[0][:, c, e * P:(e + 1) * P],
                                       vec[:, B_, c:c + 1], start=(c == 0), stop=(c == DT - 1))
                mm.then_inc(bias_sum, 1)
                pe.wait_ge(scaled, (layer + 1) * DT)
                pe.wait_ge(bias_ready, layer + 1)

            def rep_b(it, g, s):
                d, n = g // NS, g % NS
                pe.wait_ge(parts_ready, it * 2 + (d + 1))
                pe.wait_ge(v_ready, tiles(it, DT * g))
                for h in range(NH):
                    mm = pe.matmul(b_rep[:, half(h)], select[:, n, :], parts_of(d, s)[:, half(h)],
                                   start=True, stop=True)
                mm.then_inc(b_ready, 1)

            def rep_c(it, k, s):
                g, h = k // DT, k % DT
                d, n = g // NS, g % NS
                pe.wait_ge(c_ready, it * (2 * GROUPS) + k)
                if k == 0:
                    pe.wait_ge(parts_ready, it * 2 + 1)
                if k == TILES // 2:
                    pe.wait_ge(parts_ready, it * 2 + 2)
                pe.matmul(c_rep[:], select[:, NS + n, :], parts_of(d, s)[:, half(h)],
                          start=True, stop=True).then_inc(c_filled, 1)

            def add_up(it, k):
                c = k % DT
                pe.wait_ge(p_ready, tiles(it, k + 1))
                if k == 0:
                    pe.wait_ge(gated, it)
                for h in range(NH):
                    mm = pe.matmul(y[:, c, half(h)], ident[:], ring[k % NR][:, half(h)],
                                   start=(k < DT), stop=(k >= TILES - DT), skip_group_check=True)
                mm.then_inc(summed, 1)

            def over_channels(lhs, rhs, h):
                for c in range(DT):
                    mm = pe.matmul(bank[:], lhs(c), rhs[:, c, half(h)], start=(c == 0), stop=(c == DT - 1))
                return mm

            def prepare(k, n, s):
                for h in range(NH):
                    if k == (6, 9)[h]:
                        pe.wait_ge(x_loaded, (n + 1) * 16)
                        if h == 0:
                            pe.wait_ge(dtp_out, n * (2 * FILLS))
                        else:
                            pe.wait_ge(centred, n * 2 + 1)
                        over_channels(lambda c: mean_w[:], xin, h).then_inc(mean_ready, 1)
                    if k == (11, 13)[h]:
                        pe.wait_ge(squared, n * 2 + (h + 1))
                        if h == 0:
                            pe.wait_ge(centred, n * 2 + 2)
                        else:
                            pe.wait_ge(logvar, n * 2 + 1)
                        over_channels(lambda c: mean_w[:], pre, h).then_inc(var_ready, 1)
                for i, (e, h) in enumerate(layers_steps):
                    cols = slice(e * P, (e + 1) * P)
                    if k == 14 + i:
                        pe.wait_ge(normed, n * 2 + (h + 1))
                        pe.wait_ge(xp_ready, n * FILLS + i)
                        if i == 0:
                            pe.wait_ge(logvar, n * 2 + 2)
                        over_channels(lambda c: wt[0][:, c, cols], w[s], h).then_inc(proj_ready, 1)
                    for d in range(DIRS):
                        if k == (19, 43)[d] + i:
                            pe.wait_ge(conv_out, n * (2 * FILLS) + (d * FILLS + i))
                            if i == 0 and d == 0:
                                pe.wait_ge(xp_ready, (n + 1) * FILLS)
                            if i == 0 and d == 1:
                                pe.wait_ge(dtp_out, n * (2 * FILLS) + FILLS)
                            over_channels(lambda c: wt[1 + d][:, c, cols], xp, h).then_inc(conv_ready, 1)
                        if k == (31, 53)[d] + i:
                            if i == 0:
                                pe.wait_ge(dbc_out, n * 4 + (2 * d + 2))
                            pe.wait_ge(dtp_out, n * (2 * FILLS) + (d * FILLS + i))
                            pe.matmul(bank[:], wt_dbc[:, DT + e, :], dbc[:, half(h)],
                                      start=True, stop=True).then_inc(dtp_ready, 1)
                for d in range(DIRS):
                    for h in range(NH):
                        if k == (29, 51)[d] + h:
                            pe.wait_ge(xs_ready, n * 2 + (d + 1))
                            if h == 0:
                                pe.wait_ge(conv_out, n * (2 * FILLS) + (d + 1) * FILLS)
                            else:
                                pe.wait_ge(dbc_out, n * 4 + (2 * d + 1))
                            over_channels(lambda c: wt_dbc[:, c, :], xs_of(d, s), h).then_inc(dbc_ready, 1)

            fills = {6, 9, 11, 13, *range(14, 18), *range(19, 23), *range(29, 35), *range(43, 47), *range(51, 57)}
            lag, now, run = [], LAG0, 0
            for k in range(TILES):
                run = run + 1 if (k in fills) == (k - 1 in fills) else 1
                if k in fills and run % 2 == 1:
                    now = min(now + 1, LAG_MOST)
                elif k > LAG0 and k not in fills and run % 2 == 0:
                    now = max(now - 1, LAG_LEAST if k < 57 else LAG0)
                if k >= 60:
                    now = LAG0
                lag.append(now)

            def add_due(it, k):
                for t in range(k - lag[k - 1], k - lag[k] + 1):
                    if t >= 0:
                        add_up(it, t)
                    elif not (isinstance(it, int) and it == 0):
                        add_up(it - 1, t + TILES)

            def slots(it, s, k0, k1, more):
                for k in range(k0, k1):
                    if k == 0:
                        rep_b(it, 0, s)
                    if k % DT == 0 and k + DT < TILES:
                        rep_b(it, k // DT + 1, s)
                    if k + C_LEAD < TILES:
                        rep_c(it, k + C_LEAD, s)
                    elif more:
                        rep_c(it + 1, k + C_LEAD - TILES, 1 - s)
                    add_due(it, k)
                    if more:
                        prepare(k, it + 1, 1 - s)

            def tail(it, s):
                for k in range(TILES - LAG0, TILES):
                    add_up(it, k)

            def begin():
                for k in range(C_LEAD):
                    rep_c(0, k, 0)

            run_layers(weights, slots, prepare, begin, tail, nothing, pe)

        @block.vector
        def _(dve):
            dve.sem_inc(v_ready, SEED)
            dve.sem_inc(h_ready, SEED)

            def weights(layer, n):
                dve.wait_ge(raw_loaded, (layer + 1) * (16 * RAW_DMAS))
                dve.wait_ge(delta_ready, n * 2)
                dve.wait_ge(dxz_ready, n * 2)
                nc.vector.tensor_copy(vec[:], raw_vec[:]).then_inc(vec_copied, 1)
                dve.wait_ge(a_exp, layer + 1)
                nc.vector.tensor_scalar(a_cur[:], a_cur[:], -1.0, None, ALU.mult).then_inc(a_neg, 1)
                dve.wait_ge(bias_sum, layer + 1)
                dve.wait_ge(vec_copied, layer + 1)
                nc.vector.tensor_tensor(pbias[:], bank[:, 0:DT], vec[:, PB_, :], ALU.add).then_inc(bias_ready, 1)
                for c in range(DT):
                    nc.vector.tensor_scalar(wt[0][:, c, :], wt[0][:, c, :], vec[:, G_, c:c + 1], None,
                                            ALU.mult).then_inc(scaled, 1)

            def times_b(it, k, s):
                d, c = k // (NS * DT), k % DT
                if k % (TILES // 2) == 0:
                    dve.wait_ge(u_ready, it * 2 + (d + 1))
                dve.wait_ge(b_ready, it * GROUPS + (k // DT + 1))
                dve.wait_ge(summed, tiles(it, k + 1 - NR))
                nc.vector.tensor_tensor(ring[k % NR][:], u_of(d, s)[:, c, :], b_rep[:], ALU.mult).then_inc(v_ready, 1)

            def scan(it, k):
                d = k // (NS * DT)
                dve.wait_ge(v_ready, tiles(it, k + 1))
                dve.wait_ge(da_ready, tiles(it, k + 1))
                a, b = dA[k % NDA][:], ring[k % NR][:]
                if d:
                    a, b = a[:, ::-1], b[:, ::-1]
                nc.vector.tensor_tensor_scan(b, a, b, 0.0, ALU.mult, ALU.add).then_inc(h_ready, 1)

            def finish(it, s):
                dve.wait_ge(summed, tiles(it, TILES))
                nc.vector.tensor_tensor(z[s][:], y[:], z[s][:], ALU.mult).then_inc(gated, 1)
                dve.wait_ge(gated, it + 1)
                dve.wait_ge(w_ready, it + 1)
                nc.vector.tensor_tensor(z[s][:], z[s][:], w[s][:], ALU.add).then_inc(out_ready, 1)

            def prepare(k, n, s):
                for h in range(NH):
                    if k == (8, 10)[h]:
                        dve.wait_ge(mean_ready, n * 2 + (h + 1))
                        if not isinstance(n, int):
                            dve.wait_ge(out_ready, n - 1)
                        nc.vector.tensor_tensor(w[s][:, :, half(h)], xin[:, :, half(h)],
                                                bank[:].unsqueeze(1).to_broadcast([P, DT, HALF]),
                                                ALU.subtract).then_inc(centred, 1)
                if k == 22:
                    dve.wait_ge(ln_done, n * CHAINS + 1)
                    nc.vector.scalar_tensor_tensor(tmp[:], xp[:], 0.0, tmp[:], ALU.min,
                                                   ALU.subtract).then_inc(gate_log, 1)
                for d in range(DIRS):
                    if k == (28, 50)[d]:
                        dve.wait_ge(ln_done, n * CHAINS + (conv_chain[d] + 1))
                        dve.wait_ge(u_ready, n * 2 + d)
                        dve.wait_ge(w_ready, n)
                        nc.vector.scalar_tensor_tensor(xs_of(d, s)[:], pre[:], 0.0, tmp[:], ALU.max,
                                                       ALU.add).then_inc(xs_ready, 1)
                    if k == (42, 61)[d]:
                        dve.wait_ge(ln_done, n * CHAINS + (delta_chain[d] + 1))
                        nc.vector.scalar_tensor_tensor(delta_of(d, s)[:], pre[:], 0.0, tmp[:], ALU.max,
                                                       ALU.add).then_inc(delta_ready, 1)
                for d in range(DIRS):
                    if k == (38, 58)[d]:
                        dve.wait_ge(mid_ready, n * 4 + (2 * d + 2))
                        ps, rows = parts_of(d, s), slice(2 * BC, 3 * BC)
                        nc.vector.tensor_tensor(ps[rows, :], tmp[rows, 0, :], ps[rows, :],
                                                ALU.subtract).then_inc(parts_ready, 1)
                if k == 56:
                    nc.vector.tensor_copy(a_step[s][:], a_cur[:]).then_inc(a_ready, 1)
                if k == 57:
                    dve.wait_ge(xsum_ready, n + 1)
                    dve.wait_ge(gate_ready, n + 1)
                    for c in range(DT):
                        nc.vector.scalar_tensor_tensor(xf[:, c, :], xf[:, c, :], vec[:, DP_, c:c + 1],
                                                       z[s][:, c, :], ALU.mult, ALU.mult).then_inc(dxz_ready, 1)

            def slots(it, s, k0, k1, more):
                for g in range(k0 // DT, k1 // DT):
                    for c in range(DT):
                        times_b(it, g * DT + c, s)
                    for c in range(DT):
                        scan(it, g * DT + c)
                    if g == FINISH and not (isinstance(it, int) and it == 0):
                        finish(it - 1, 1 - s)
                    if more:
                        for c in range(DT):
                            prepare(g * DT + c, it + 1, 1 - s)

            run_layers(weights, slots, prepare, nothing, finish, nothing, dve)


_INS = ['x'] + ['L0_conv_' + n for n in ('ln_g', 'ln_b', 'proj_w', 'proj_b', 'convf_w', 'convf_b', 'convb_w',
                                         'convb_b', 'dbc_w', 'dtp_w', 'dtp_b', 'A_log', 'D_param')]
_OUTS = [((8, 256, 32, 32), 'float32')]


def kernel(**inputs):
    import numpy as _np
    import concourse.bacc as _bacc
    from concourse import mybir as _mybir
    from concourse.bass_utils import run_bass_kernel_spmd as _run

    nc = _bacc.Bacc("TRN2", target_bir_lowering=False, num_devices=1)
    arrays, args = {}, []
    for name in _INS:
        a = _np.ascontiguousarray(inputs[name])
        arrays[f"in_{name}_dram"] = a
        args.append(nc.dram_tensor(f"in_{name}_dram", a.shape, _mybir.dt.from_np(a.dtype), kind="ExternalInput").ap())
    for i, (shape, dtype) in enumerate(_OUTS):
        dt = _mybir.dt.from_np(_np.dtype(dtype))
        args.append(nc.dram_tensor(f"out_{i}_dram", shape, dt, kind="ExternalOutput").ap())
    conv_seq_kernel(nc, *args)
    r = _run(nc, [arrays], core_ids=[0])
    got = tuple(r.results[0][f"out_{i}_dram"] for i in range(len(_OUTS)))
    return got[0]
```

```python
from contextlib import ExitStack

import concourse.bass as bass
from concourse import mybir
from concourse.alu_op_type import AluOpType as ALU

ACT = mybir.ActivationFunctionType
F32 = mybir.dt.float32
BF16 = mybir.dt.bfloat16

P = 128
HALF = 512
EPS = 1e-5
TABLES = "natural_log_exp_and_others"


def conv_seq_kernel(nc, x, ln_g, ln_b, proj_w, proj_b, convf_w, convf_b, convb_w, convb_b,
                    dbc_w, dtp_w, dtp_b, A_log, D_param, out):
    LAYERS, D = ln_g.shape
    NB, _, HH, WW = x.shape
    T = HH * WW
    DT = D // P
    NH = T // HALF
    RANK = dtp_w.shape[2]
    NS = A_log.shape[2]
    BC = 2 * NS
    DIRS = 2
    GROUPS = DIRS * NS
    TILES = GROUPS * DT
    FILLS = DT * NH
    assert DT == 2 and NH == 2 and BC == 32 and RANK == 32 and NB % 2 == 0

    NDA, NR, NC = 4, 8, 4
    SEED = 8
    LAG0, LAG_LEAST, LAG_MOST = 5, 2, 5
    FIRST = 6
    PARTS = 6
    PE_TURNS = (0, 1, 3, 4)
    ACT_TURNED = (0, 1, 3, 5)
    PE_BIAS = 4
    CONV_AT = ((19, 20, 22, 24), (43, 44, 45, 46))
    FINISH = 2
    AHEAD = 3
    N_VEC = 7
    G_, B_, PB_, CFB_, CBB_, DTB_, DP_ = range(N_VEC)
    RAW_DMAS = 4 + 1 + 1 + N_VEC

    x_d = x.rearrange("b (c p) h w -> b p c (h w)", p=P)
    out_d = out.rearrange("b (c p) h w -> b p c (h w)", p=P)

    with ExitStack() as ctx:
        def sb(name, shape, dt=F32):
            return ctx.enter_context(nc.sbuf_tensor(name, shape, dt))

        def sem(name):
            return ctx.enter_context(nc.semaphore(name))

        y = ctx.enter_context(nc.psum_tensor("y", [P, DT, T], F32))
        b_rep = ctx.enter_context(nc.psum_tensor("b_rep", [P, T], F32))
        bank = [ctx.enter_context(nc.psum_tensor(f"bank{i}", [P, HALF], F32)) for i in range(2)]

        w = [sb(f"w{s}", [P, DT, T]) for s in range(2)]
        z = [sb(f"z{s}", [P, DT, T]) for s in range(2)]
        delta0 = sb("delta0", [P, DT, T])
        u0 = sb("u0", [P, DT, T])
        parts0 = sb("parts0", [P, T], BF16)
        delta1 = [sb(f"delta1_{s}", [P, DT, T]) for s in range(2)]
        u1 = [sb(f"u1_{s}", [P, DT, T]) for s in range(2)]
        parts1 = [sb(f"parts1_{s}", [P, T], BF16) for s in range(2)]
        a_step = [sb(f"a_step{s}", [P, DT, NS]) for s in range(2)]
        tmp = sb("tmp", [P, DT, T])
        xp = sb("xp", [P, DT, T])
        pre = sb("pre", [P, DT, T])
        xf = sb("xf", [P, DT, T])
        dbc = sb("dbc", [P, T])

        def delta_of(d, s):
            return delta1[s] if d else delta0

        def u_of(d, s):
            return u1[s] if d else u0

        def parts_of(d, s):
            return parts1[s] if d else parts0

        def xs_of(d, s):
            return w[s] if d else xf

        dA = [sb(f"dA{i}", [P, T]) for i in range(NDA)]
        ring = [sb(f"ring{i}", [P, T]) for i in range(NR)]
        c_sb = [sb(f"c{i}", [P, T]) for i in range(NC)]

        raw_w = sb("raw_w", [P, DT, D])
        raw_dbc = sb("raw_dbc", [P, D])
        raw_dtp = sb("raw_dtp", [P, DT, P])
        raw_vec = sb("raw_vec", [P, N_VEC, DT])
        raw_a = sb("raw_a", [P, DT, NS])
        wt = [sb(f"wt{i}", [P, DT, D]) for i in range(3)]
        wt_dbc = sb("wt_dbc", [P, 2 * DT, P])
        vec = sb("vec", [P, N_VEC, DT])
        pbias = sb("pbias", [P, DT])
        a_cur = sb("a_cur", [P, DT, NS])
        ident = sb("ident", [P, P])
        diag_d = sb("diag_d", [P, DT, P])
        mean_w = sb("mean_w", [P, P])
        select = sb("select", [P, NS, P], BF16)
        eps = sb("eps", [P, 1])

        c_rows = nc.dram_tensor("c_rows", (2, DIRS, NS, T), F32, kind="Internal").ap()

        consts_clear = sem("consts_clear")
        consts_ready = sem("consts_ready")
        raw_loaded = sem("raw_loaded")
        square_loaded = sem("square_loaded")
        vec_copied = sem("vec_copied")
        turned = sem("turned")
        turned_out = sem("turned_out")
        bias_sum = sem("bias_sum")
        bias_ready = sem("bias_ready")
        a_exp = sem("a_exp")
        a_neg = sem("a_neg")
        scaled = sem("scaled")

        x_loaded = sem("x_loaded")
        stored = sem("stored")
        mean_ready = sem("mean_ready")
        centred = sem("centred")
        squared = sem("squared")
        var_ready = sem("var_ready")
        logvar = sem("logvar")
        rstd_ready = sem("rstd_ready")
        normed = sem("normed")
        proj_ready = sem("proj_ready")
        xp_ready = sem("xp_ready")
        conv_ready = sem("conv_ready")
        conv_out = sem("conv_out")
        abs_done = sem("abs_done")
        exp_done = sem("exp_done")
        ln_done = sem("ln_done")
        gate_log = sem("gate_log")
        gate_sig = sem("gate_sig")
        gate_ready = sem("gate_ready")
        xs_ready = sem("xs_ready")
        dbc_ready = sem("dbc_ready")
        dbc_out = sem("dbc_out")
        dtp_ready = sem("dtp_ready")
        dtp_out = sem("dtp_out")
        hi_ready = sem("hi_ready")
        rest_ready = sem("rest_ready")
        mid_ready = sem("mid_ready")
        parts_ready = sem("parts_ready")
        delta_ready = sem("delta_ready")
        u_ready = sem("u_ready")
        diag_ready = sem("diag_ready")
        skip_summed = sem("skip_summed")
        w_loaded = sem("w_loaded")
        a_ready = sem("a_ready")
        gated = sem("gated")
        out_ready = sem("out_ready")

        da_ready = sem("da_ready")
        v_ready = sem("v_ready")
        h_ready = sem("h_ready")
        p_ready = sem("p_ready")
        summed = sem("summed")
        b_ready = sem("b_ready")
        c_stored = sem("c_stored")
        c_loaded = [sem(f"c_loaded{i}") for i in range(NC)]

        def tiles(it, k):
            return it * TILES + (SEED + k)

        CHAINS = 5
        conv_chain = [1, 3]
        delta_chain = [2, 4]

        layers_steps = [(e, h) for h in range(NH) for e in range(DT)]

        def half(h):
            return slice(h * HALF, (h + 1) * HALF)

        def early(it, n):
            return isinstance(it, int) and it < n

        block = ctx.enter_context(nc.Block())

        def run_layers(weights, slots, prepare, begin, tail, load_raw, e, first=FIRST):
            def no_weights(part):
                pass

            def turn(it, s, more, next_weights=no_weights):
                slots(it, s, first, TILES, more > 0, no_weights)
                if more:
                    slots(it + 1, 1 - s, 0, first, more > 1, next_weights)
                else:
                    tail(it, s)

            load_raw(0)
            for part in range(PARTS):
                weights(part, 0, 0)
            for k in range(TILES):
                prepare(k, 0, 0)
            begin()
            slots(0, 0, 0, first, True, no_weights)
            with e.Fori(0, LAYERS - 1) as layer:
                load_raw(layer + 1)
                with e.Fori(0, NB // 2 - 1) as pair:
                    it = layer * NB + pair * 2
                    turn(it, 0, 2)
                    turn(it + 1, 1, 2)
                it = layer * NB + (NB - 2)
                turn(it, 0, 2, lambda part: weights(part, layer + 1, it + 2))
                turn(it + 1, 1, 2)
            last = (LAYERS - 1) * NB
            with e.Fori(0, NB // 2 - 1) as pair:
                it = pair * 2 + last
                turn(it, 0, 2)
                turn(it + 1, 1, 2)
            turn(last + NB - 2, 0, 1)
            turn(last + NB - 1, 1, 0)

        def nothing(*_):
            pass

        @block.sync
        def _(sp):
            def load_c(it, g, s):
                sp.wait_ge(p_ready, tiles(it, DT * (g + 1 - NC)))
                sp.dma_start(c_sb[g % NC][:], c_rows[s, g // NS, g % NS:g % NS + 1, :].to_broadcast([P, T])
                             ).then_inc(c_loaded[g % NC], 16)

            def load_x(n, src, b):
                sp.wait_ge(delta_ready, n * 2)
                sp.dma_start(pre[:], src[b]).then_inc(x_loaded, 16)

            def load_w(it, src, s, b):
                sp.wait_ge(skip_summed, it * (DIRS * DT) + DIRS * DT)
                sp.dma_start(w[s][:], src[b]).then_inc(w_loaded, 16)

            def store(it, s, b):
                sp.wait_ge(out_ready, it + 1)
                sp.dma_start(out_d[b], z[s][:]).then_inc(stored, 16)

            def step(it, b, src, next_src, more=True):
                s = b % 2
                for g in range(GROUPS):
                    if early(it, 1) and g % NS == 0:
                        sp.wait_ge(c_stored, 16 * (g // NS + 1))
                    load_c(it, g, s)
                    if g == 3 and more:
                        load_x(it + 1, next_src, (b + 1) % NB)
                    if g == 7 and not early(it, 1):
                        store(it - 1, 1 - s, (b - 1) % NB)
                    if g == 24:
                        load_w(it, src, s, b)

            load_x(0, x_d, 0)
            for b in range(NB):
                step(b, b, x_d, x_d if b < NB - 1 else out_d)
            with sp.Fori(1, LAYERS - 1) as layer:
                for b in range(NB):
                    step(layer * NB + b, b, out_d, out_d)
            last = (LAYERS - 1) * NB
            for b in range(NB):
                step(last + b, b, out_d, out_d, b < NB - 1)
            store(last + NB - 1, 1, NB - 1)
            sp.wait_ge(stored, 16 * (last + NB))

        @block.gpsimd
        def _(pool):
            nc.gpsimd.memset(ident[:], 0.0).then_inc(consts_clear, 1)
            nc.gpsimd.memset(select[:], 0.0).then_inc(consts_clear, 1)
            nc.gpsimd.memset(raw_dtp[:], 0.0).then_inc(consts_ready, 1)
            nc.gpsimd.memset(mean_w[:], 1.0 / D).then_inc(consts_ready, 1)
            nc.gpsimd.memset(eps[:], EPS).then_inc(consts_ready, 1)
            pool.wait_ge(consts_clear, 2)
            nc.gpsimd.affine_select(out=ident[:], in_=ident[:], compare_op=ALU.not_equal, fill=1.0,
                                    base=0, pattern=[[-1, P]], channel_multiplier=1).then_inc(consts_ready, 1)
            for part in range(3):
                pool.wait_ge(consts_clear, 2 + part)
                nc.gpsimd.affine_select(out=select[:], in_=select[:], compare_op=ALU.not_equal, fill=1.0,
                                        base=-BC * part, pattern=[[-1, NS], [0, P]],
                                        channel_multiplier=1).then_inc(consts_clear, 1)
            pool.wait_ge(consts_clear, 5)
            pool.sem_inc(consts_ready, 1)
            pool.sem_inc(p_ready, SEED)

            def product(it, k, s):
                g = k // DT
                pool.wait_ge(h_ready, tiles(it, k + 1))
                pool.wait_ge(c_loaded[g % NC], it * (16 * GROUPS // NC) + (16 * (g // NC) + 16))
                nc.gpsimd.tensor_tensor(ring[k % NR][:], ring[k % NR][:], c_sb[g % NC][:],
                                        ALU.mult).then_inc(p_ready, 1)

            def prepare(k, n, s):
                for h in range(NH):
                    if k == 13 + 2 * h:
                        pool.wait_ge(rstd_ready, n * 2 + (h + 1))
                        pool.wait_ge(centred, n * 2 + (h + 1))
                        wh = w[s][:, :, half(h)]
                        nc.gpsimd.tensor_tensor(wh, wh, tmp[:, 0:1, half(h)].to_broadcast([P, DT, HALF]),
                                                ALU.mult).then_inc(normed, 1)
                if k == 24:
                    pool.wait_ge(gate_sig, n + 1)
                    if not early(n, 2):
                        pool.wait_ge(stored, (n - 1) * 16)
                    nc.gpsimd.tensor_tensor(z[s][:], xp[:], tmp[:], ALU.mult).then_inc(gate_ready, 1)
                for d in range(DIRS):
                    ps = parts_of(d, s)
                    if k == (45, 63)[d]:
                        pool.wait_ge(c_stored, n * 32 + (16 * d + 16))
                    if k == (35, 55)[d]:
                        pool.wait_ge(hi_ready, n * 2 + (d + 1))
                        pool.wait_ge(xs_ready, n * 2 + (d + 1))
                        nc.gpsimd.tensor_tensor(tmp[:, 0, :], dbc[:], ps[:], ALU.subtract).then_inc(rest_ready, 1)
                    if k == (43, 63)[d]:
                        pool.wait_ge(delta_ready, n * 2 + (d + 1))
                        if d == 0 and not early(n, 1):
                            pool.wait_ge(v_ready, tiles(n - 1, TILES // 2))
                        nc.gpsimd.tensor_tensor(u_of(d, s)[:], delta_of(d, s)[:], xs_of(d, s)[:],
                                                ALU.mult).then_inc(u_ready, 1)

            def finish(it, s):
                pool.wait_ge(gated, it + 1)
                pool.wait_ge(w_loaded, it * 16 + 16)
                nc.gpsimd.tensor_tensor(z[s][:], z[s][:], w[s][:], ALU.add).then_inc(out_ready, 1)

            def slots(it, s, k0, k1, more, weights):
                for k in range(k0, k1):
                    product(it, k, s)
                    if k == FIRST - 1 and not early(it, 1):
                        finish(it - 1, 1 - s)
                    if more:
                        prepare(k, it + 1, 1 - s)

            run_layers(nothing, slots, prepare, nothing, finish, nothing, pool)

        @block.scalar
        def _(act):
            nc.scalar.preload_act_table_set(TABLES)
            act.sem_inc(da_ready, SEED)
            act.wait_ge(consts_ready, 5)

            def load_square(j, one):
                wd = (proj_w, convf_w, convb_w)[j]
                act.dma_start(raw_w[:], wd[one].rearrange("o (c p) d -> p (o c) d", p=P)).then_inc(square_loaded, 16)

            def load_raw(layer):
                act.wait_ge(turned_out, layer * 4)
                act.wait_ge(vec_copied, layer)
                act.wait_ge(a_exp, layer)
                one = slice(layer, layer + 1) if isinstance(layer, int) else bass.ds(layer, 1)
                load_square(0, one)
                rows = dbc_w[one].rearrange("o e d -> (o e) d")
                for part in range(3):
                    act.dma_start(raw_dbc[BC * part:BC * (part + 1), :], rows[RANK:RANK + BC, :]).then_inc(raw_loaded, 16)
                act.dma_start(raw_dbc[3 * BC:3 * BC + RANK, :], rows[0:RANK, :]).then_inc(raw_loaded, 16)
                act.dma_start(raw_dtp[:, :, P - RANK:P],
                              dtp_w[one].rearrange("o (c p) r -> p (o c) r", p=P)).then_inc(raw_loaded, 16)
                act.dma_start(raw_a[:], A_log[one].rearrange("o (c p) n -> p (o c) n", p=P)).then_inc(raw_loaded, 16)
                for i, vd in enumerate((ln_g, ln_b, proj_b, convf_b, convb_b, dtp_b, D_param)):
                    act.dma_start(raw_vec[:, i, :], vd[one].rearrange("o (c p) -> p (o c)", p=P),
                                  allow_slow_non_contiguous=True).then_inc(raw_loaded, 16)

            def weights(part, layer, n):
                one = slice(layer, layer + 1) if isinstance(layer, int) else bass.ds(layer, 1)

                def copy_turned(j):
                    act.wait_ge(turned, layer * 4 + (j + 1))
                    if j in (0, 2):
                        load_square(j // 2 + 1, one)
                    dst = (wt[0], wt_dbc, wt[1], wt[2])[j]
                    nc.scalar.copy(dst[:].rearrange("p c d -> p (c d)"), bank[j % 2][:]).then_inc(turned_out, 1)

                if part == 0:
                    act.wait_ge(raw_loaded, (layer + 1) * (16 * RAW_DMAS))
                    act.wait_ge(a_ready, n)
                    nc.scalar.activation(a_cur[:], raw_a[:], ACT.Exp).then_inc(a_exp, 1)
                for j in range(4):
                    if part == ACT_TURNED[j]:
                        copy_turned(j)
                if part == PARTS - 1:
                    act.wait_ge(vec_copied, layer + 1)
                    act.wait_ge(bias_ready, layer + 1)

            def tile_exp(it, k, s):
                d, n, c = k // (NS * DT), (k // DT) % NS, k % DT
                if k == 0:
                    act.wait_ge(a_ready, it + 1)
                if k % (TILES // 2) == 0:
                    act.wait_ge(delta_ready, it * 2 + (d + 1))
                act.wait_ge(h_ready, tiles(it, k + 1 - NDA))
                nc.scalar.activation(dA[k % NDA][:], delta_of(d, s)[:, c, :], ACT.Exp,
                                     scale=a_step[s][:, c, n:n + 1]).then_inc(da_ready, 1)

            def abs_exp(chain, n, src):
                nc.scalar.activation(tmp[:], src[:], ACT.Abs).then_inc(abs_done, 1)
                act.wait_ge(abs_done, n * CHAINS + (chain + 1))
                nc.scalar.activation(tmp[:], tmp[:], ACT.Exp, scale=-1.0).then_inc(exp_done, 1)

            def log1p(chain, n):
                act.wait_ge(exp_done, n * CHAINS + (chain + 1))
                nc.scalar.activation(tmp[:], tmp[:], ACT.Ln, bias=1.0).then_inc(ln_done, 1)

            def prepare(k, n, s):
                if k in (12, 14):
                    rstd(n, (k - 12) // 2)
                for h in range(NH):
                    if k == 10 + 2 * h:
                        act.wait_ge(centred, n * 2 + (h + 1))
                        nc.scalar.activation(pre[:, :, half(h)], w[s][:, :, half(h)], ACT.Square).then_inc(squared, 1)
                for i, (e, h) in enumerate(layers_steps):
                    if k == 15 + i:
                        act.wait_ge(proj_ready, n * FILLS + (i + 1))
                        nc.scalar.activation(xp[:, e, half(h)], bank[i % 2][:], ACT.Identity,
                                             bias=pbias[:, e:e + 1]).then_inc(xp_ready, 1)
                if k == 19:
                    act.wait_ge(xp_ready, n * FILLS + FILLS)
                    act.wait_ge(normed, n * 2 + 2)
                    abs_exp(0, n, xp)
                if k == 20:
                    log1p(0, n)
                if k == 23:
                    act.wait_ge(gate_log, n + 1)
                    nc.scalar.activation(tmp[:], tmp[:], ACT.Exp).then_inc(gate_sig, 1)
                for d in range(DIRS):
                    for i, (e, h) in enumerate(layers_steps):
                        if k == CONV_AT[d][i] + 1:
                            act.wait_ge(conv_ready, n * (2 * FILLS) + (d * FILLS + i + 1))
                            if d == 0:
                                act.wait_ge(var_ready, n * 2 + 2)
                            else:
                                act.wait_ge(delta_ready, n * 2 + 1)
                            nc.scalar.activation(pre[:, e, half(h)], bank[i % 2][:], ACT.Identity,
                                                 bias=vec[:, CFB_ + d, e:e + 1]).then_inc(conv_out, 1)
                    if k == (26, 47)[d]:
                        act.wait_ge(conv_out, n * (2 * FILLS) + (d + 1) * FILLS)
                        if d == 0:
                            act.wait_ge(gate_ready, n + 1)
                        else:
                            act.wait_ge(delta_ready, n * 2 + 1)
                        abs_exp(conv_chain[d], n, pre)
                    if k == (27, 48)[d]:
                        log1p(conv_chain[d], n)
                    for h in range(NH):
                        if k == (32, 52)[d] + h:
                            act.wait_ge(dbc_ready, n * 4 + (2 * d + h + 1))
                            act.wait_ge(parts_ready, n * 2 + d)
                            act.wait_ge(c_stored, n * 32 + 16 * d)
                            nc.scalar.copy(dbc[:, half(h)], bank[h][:]).then_inc(dbc_out, 1)
                    for i, (e, h) in enumerate(layers_steps):
                        if k == (34, 54)[d] + i:
                            act.wait_ge(dtp_ready, n * (2 * FILLS) + (d * FILLS + i + 1))
                            act.wait_ge(xs_ready, n * 2 + (d + 1))
                            nc.scalar.activation(pre[:, e, half(h)], bank[i % 2][:], ACT.Identity,
                                                 bias=vec[:, DTB_, e:e + 1]).then_inc(dtp_out, 1)
                    ps = parts_of(d, s)
                    if k == (34, 54)[d]:
                        act.wait_ge(dbc_out, n * 4 + (2 * d + 2))
                        nc.scalar.copy(ps[:], dbc[:]).then_inc(hi_ready, 1)
                        if not early(n, 1):
                            act.wait_ge(p_ready, tiles(n - 1, 0))
                        act.dma_start(c_rows[s, d], dbc[NS:2 * NS, :]).then_inc(c_stored, 16)
                    if k == (37, 57)[d]:
                        act.wait_ge(rest_ready, n * 2 + (d + 1))
                        for rows in (slice(BC, 2 * BC), slice(2 * BC, 3 * BC)):
                            nc.scalar.copy(ps[rows, :], tmp[rows, 0, :]).then_inc(mid_ready, 1)
                    if k == (39, 59)[d]:
                        act.wait_ge(dtp_out, n * (2 * FILLS) + (d + 1) * FILLS)
                        act.wait_ge(parts_ready, n * 2 + (d + 1))
                        abs_exp(delta_chain[d], n, pre)
                    if k == (40, 60)[d]:
                        log1p(delta_chain[d], n)

                if k == 41:
                    act.wait_ge(skip_summed, n * (DIRS * DT))
                    for c in range(DT):
                        nc.scalar.activation(diag_d[:, c, :], ident[:], ACT.Copy,
                                             scale=vec[:, DP_, c:c + 1]).then_inc(diag_ready, 1)

            def rstd(n, h):
                act.wait_ge(var_ready, n * 2 + (h + 1))
                act.wait_ge(delta_ready, n * 2)
                th = tmp[:, 0, half(h)]
                nc.scalar.activation(th, bank[h][:], ACT.Ln, bias=eps[:, 0:1]).then_inc(logvar, 1)
                act.wait_ge(logvar, n * 2 + (h + 1))
                nc.scalar.activation(th, th, ACT.Exp, scale=-0.5).then_inc(rstd_ready, 1)

            def slots(it, s, k0, k1, more, weights):
                for k in range(k0, k1):
                    tile_exp(it, k, s)
                    weights(k - AHEAD)
                    if more:
                        prepare(k - AHEAD, it + 1, 1 - s)

            run_layers(weights, slots, prepare, nothing, nothing, load_raw, act, FIRST + AHEAD)

        @block.tensor
        def _(pe):
            pe.sem_inc(summed, SEED)
            pe.wait_ge(consts_ready, 5)

            def weights(part, layer, n):
                for j in range(4):
                    if part != PE_TURNS[j]:
                        continue
                    if j == 0:
                        pe.wait_ge(raw_loaded, (layer + 1) * (16 * RAW_DMAS))
                        pe.wait_ge(dtp_out, n * (2 * FILLS))
                    if j > 1:
                        pe.wait_ge(turned_out, layer * 4 + (j - 1))
                    if j != 1:
                        pe.wait_ge(square_loaded, layer * 48 + (0, 0, 1, 2)[j] * 16 + 16)
                    for q in range(4):
                        if j != 1:
                            src = raw_w[:, q % DT, (q // DT) * P:(q // DT + 1) * P]
                        else:
                            src = raw_dbc[:, q * P:(q + 1) * P] if q < DT else raw_dtp[:, q - DT, :]
                        mm = pe.transpose(bank[j % 2][:, q * P:(q + 1) * P], src, ident[:])
                    mm.then_inc(turned, 1)
                if part == PE_BIAS:
                    pe.wait_ge(turned_out, layer * 4 + 3)
                    pe.wait_ge(vec_copied, layer + 1)
                    for e in range(DT):
                        for c in range(DT):
                            mm = pe.matmul(bank[0][:, e:e + 1], wt[0][:, c, e * P:(e + 1) * P],
                                           vec[:, B_, c:c + 1], start=(c == 0), stop=(c == DT - 1))
                    mm.then_inc(bias_sum, 1)
                if part == PARTS - 1:
                    pe.wait_ge(turned_out, layer * 4 + 4)
                    pe.wait_ge(scaled, (layer + 1) * DT)
                    pe.wait_ge(bias_ready, layer + 1)

            def rep_b(it, g, s):
                d, n = g // NS, g % NS
                pe.wait_ge(parts_ready, it * 2 + (d + 1))
                pe.wait_ge(v_ready, tiles(it, DT * g))
                for h in range(NH):
                    mm = pe.matmul(b_rep[:, half(h)], select[:, n, :], parts_of(d, s)[:, half(h)],
                                   start=True, stop=True)
                mm.then_inc(b_ready, 1)

            def add_up(it, k):
                c = k % DT
                pe.wait_ge(p_ready, tiles(it, k + 1))
                if k == 0:
                    pe.wait_ge(gated, it)
                for h in range(NH):
                    mm = pe.matmul(y[:, c, half(h)], ident[:], ring[k % NR][:, half(h)],
                                   start=(k < DT), stop=(k >= TILES - DT), skip_group_check=True)
                mm.then_inc(summed, 1)

            def add_skip(it, s, d, c):
                pe.wait_ge(diag_ready, it * DT + DT)
                pe.wait_ge(xs_ready, it * 2 + (d + 1))
                for h in range(NH):
                    mm = pe.matmul(y[:, c, half(h)], diag_d[:, c, :], xs_of(d, s)[:, c, half(h)],
                                   start=False, stop=False, skip_group_check=True)
                mm.then_inc(skip_summed, 1)

            def over_channels(dst, lhs, rhs, h):
                for c in range(DT):
                    mm = pe.matmul(dst[:], lhs(c), rhs[:, c, half(h)], start=(c == 0), stop=(c == DT - 1))
                return mm

            def prepare(k, n, s):
                for h in range(NH):
                    if k == (5, 7)[h]:
                        pe.wait_ge(x_loaded, (n + 1) * 16)
                        pe.wait_ge(dtp_out, n * (2 * FILLS))
                        over_channels(bank[h], lambda c: mean_w[:], pre, h).then_inc(mean_ready, 1)
                    if k == (11, 13)[h]:
                        pe.wait_ge(squared, n * 2 + (h + 1))
                        pe.wait_ge(centred, n * 2 + (h + 1))
                        over_channels(bank[h], lambda c: mean_w[:], pre, h).then_inc(var_ready, 1)
                for i, (e, h) in enumerate(layers_steps):
                    cols = slice(e * P, (e + 1) * P)
                    if k == 14 + i:
                        pe.wait_ge(normed, n * 2 + (h + 1))
                        if i < 2:
                            pe.wait_ge(logvar, n * 2 + (i + 1))
                        else:
                            pe.wait_ge(xp_ready, n * FILLS + (i - 1))
                        over_channels(bank[i % 2], lambda c: wt[0][:, c, cols], w[s], h).then_inc(proj_ready, 1)
                    for d in range(DIRS):
                        if k == CONV_AT[d][i]:
                            if i < 2:
                                if d == 0:
                                    pe.wait_ge(xp_ready, n * FILLS + (i + 3))
                                else:
                                    pe.wait_ge(dtp_out, n * (2 * FILLS) + (i + 3))
                            else:
                                pe.wait_ge(xp_ready, n * FILLS + FILLS)
                                pe.wait_ge(conv_out, n * (2 * FILLS) + (d * FILLS + i - 1))
                            over_channels(bank[i % 2], lambda c: wt[1 + d][:, c, cols], xp, h).then_inc(conv_ready, 1)
                        if k == (33, 53)[d] + i:
                            pe.wait_ge(dbc_out, n * 4 + (2 * d + 1 + (i if i < 2 else h)))
                            if i >= 2:
                                pe.wait_ge(dtp_out, n * (2 * FILLS) + (d * FILLS + i - 1))
                            pe.matmul(bank[i % 2][:], wt_dbc[:, DT + e, :], dbc[:, half(h)],
                                      start=True, stop=True).then_inc(dtp_ready, 1)
                for d in range(DIRS):
                    for h in range(NH):
                        if k == (31, 51)[d] + h:
                            pe.wait_ge(xs_ready, n * 2 + (d + 1))
                            pe.wait_ge(conv_out, n * (2 * FILLS) + (d * FILLS + 3 + h))
                            over_channels(bank[h], lambda c: wt_dbc[:, c, :], xs_of(d, s), h).then_inc(dbc_ready, 1)

            SKIPS = (8, 9, 24, 38)
            fills = {5, 7, 11, 13, *range(14, 18), *CONV_AT[0], *range(31, 37), *CONV_AT[1], *range(51, 57)}
            lag, now, run = [], LAG0, 0
            for k in range(TILES):
                run = run + 1 if (k in fills) == (k - 1 in fills) else 1
                if k in fills and run % 2 == 1:
                    now = min(now + 1, LAG_MOST)
                elif k > LAG0 and k not in fills and run % 2 == 0:
                    now = max(now - 1, LAG_LEAST if k < 57 else LAG0)
                if k >= 60:
                    now = LAG0
                lag.append(now)

            def add_due(it, k):
                for t in range(k - lag[k - 1], k - lag[k] + 1):
                    if t >= 0:
                        add_up(it, t)
                    elif not early(it, 1):
                        add_up(it - 1, t + TILES)

            def slots(it, s, k0, k1, more, weights):
                for k in range(k0, k1):
                    if k % DT == 0:
                        if k + DT < TILES:
                            rep_b(it, k // DT + 1, s)
                        elif more:
                            rep_b(it + 1, 0, 1 - s)
                    add_due(it, k)
                    if k in SKIPS:
                        i = SKIPS.index(k)
                        add_skip(it, s, i // DT, i % DT)
                    weights(k)
                    if more:
                        prepare(k, it + 1, 1 - s)

            def tail(it, s):
                for k in range(TILES - LAG0, TILES):
                    add_up(it, k)

            run_layers(weights, slots, prepare, lambda: rep_b(0, 0, 0), tail, nothing, pe)

        @block.vector
        def _(dve):
            dve.sem_inc(v_ready, SEED)
            dve.sem_inc(h_ready, SEED)

            def weights(part, layer, n):
                if part == 0:
                    dve.wait_ge(raw_loaded, (layer + 1) * (16 * RAW_DMAS))
                    dve.wait_ge(delta_ready, n * 2)
                    dve.wait_ge(diag_ready, n * DT)
                    nc.vector.tensor_copy(vec[:], raw_vec[:]).then_inc(vec_copied, 1)
                    dve.wait_ge(a_exp, layer + 1)
                    nc.vector.tensor_scalar(a_cur[:], a_cur[:], -1.0, None, ALU.mult).then_inc(a_neg, 1)
                if part == PARTS - 1:
                    dve.wait_ge(bias_sum, layer + 1)
                    dve.wait_ge(vec_copied, layer + 1)
                    nc.vector.tensor_tensor(pbias[:], bank[0][:, 0:DT], vec[:, PB_, :], ALU.add).then_inc(bias_ready, 1)
                    for c in range(DT):
                        nc.vector.tensor_scalar(wt[0][:, c, :], wt[0][:, c, :], vec[:, G_, c:c + 1], None,
                                                ALU.mult).then_inc(scaled, 1)

            def times_b(it, k, s):
                d, c = k // (NS * DT), k % DT
                if k % (TILES // 2) == 0:
                    dve.wait_ge(u_ready, it * 2 + (d + 1))
                dve.wait_ge(b_ready, it * GROUPS + (k // DT + 1))
                dve.wait_ge(summed, tiles(it, k + 1 - NR))
                nc.vector.tensor_tensor(ring[k % NR][:], u_of(d, s)[:, c, :], b_rep[:], ALU.mult).then_inc(v_ready, 1)

            def scan(it, k):
                d = k // (NS * DT)
                dve.wait_ge(v_ready, tiles(it, k + 1))
                dve.wait_ge(da_ready, tiles(it, k + 1))
                a, b = dA[k % NDA][:], ring[k % NR][:]
                if d:
                    a, b = a[:, ::-1], b[:, ::-1]
                nc.vector.tensor_tensor_scan(b, a, b, 0.0, ALU.mult, ALU.add).then_inc(h_ready, 1)

            def finish(it, s):
                dve.wait_ge(summed, tiles(it, TILES))
                nc.vector.tensor_tensor(z[s][:], y[:], z[s][:], ALU.mult).then_inc(gated, 1)

            def prepare(k, n, s):
                for h in range(NH):
                    if k == (8, 10)[h]:
                        dve.wait_ge(mean_ready, n * 2 + (h + 1))
                        if not early(n, 2):
                            dve.wait_ge(out_ready, n - 1)
                        nc.vector.tensor_tensor(w[s][:, :, half(h)], pre[:, :, half(h)],
                                                bank[h][:].unsqueeze(1).to_broadcast([P, DT, HALF]),
                                                ALU.subtract).then_inc(centred, 1)
                if k == 22:
                    dve.wait_ge(ln_done, n * CHAINS + 1)
                    nc.vector.scalar_tensor_tensor(tmp[:], xp[:], 0.0, tmp[:], ALU.min,
                                                   ALU.subtract).then_inc(gate_log, 1)
                for d in range(DIRS):
                    if k == (30, 50)[d]:
                        dve.wait_ge(ln_done, n * CHAINS + (conv_chain[d] + 1))
                        dve.wait_ge(u_ready, n * 2 + d)
                        if d == 0 and not early(n, 1):
                            dve.wait_ge(skip_summed, n * (DIRS * DT) - DT)
                        nc.vector.scalar_tensor_tensor(xs_of(d, s)[:], pre[:], 0.0, tmp[:], ALU.max,
                                                       ALU.add).then_inc(xs_ready, 1)
                    if k == (42, 62)[d]:
                        dve.wait_ge(ln_done, n * CHAINS + (delta_chain[d] + 1))
                        nc.vector.scalar_tensor_tensor(delta_of(d, s)[:], pre[:], 0.0, tmp[:], ALU.max,
                                                       ALU.add).then_inc(delta_ready, 1)
                for d in range(DIRS):
                    if k == (38, 58)[d]:
                        dve.wait_ge(mid_ready, n * 4 + (2 * d + 2))
                        ps, rows = parts_of(d, s), slice(2 * BC, 3 * BC)
                        nc.vector.tensor_tensor(ps[rows, :], tmp[rows, 0, :], ps[rows, :],
                                                ALU.subtract).then_inc(parts_ready, 1)
                if k == 56:
                    nc.vector.tensor_copy(a_step[s][:], a_cur[:]).then_inc(a_ready, 1)

            def slots(it, s, k0, k1, more, weights):
                for g in range(k0 // DT, k1 // DT):
                    for c in range(DT):
                        times_b(it, g * DT + c, s)
                    for c in range(DT):
                        scan(it, g * DT + c)
                    if g == FINISH and not early(it, 1):
                        finish(it - 1, 1 - s)
                    for c in range(DT):
                        weights(g * DT + c)
                    if more:
                        for c in range(DT):
                            prepare(g * DT + c, it + 1, 1 - s)

            run_layers(weights, slots, prepare, nothing, finish, nothing, dve)


_INS = ['x'] + ['L0_conv_' + n for n in ('ln_g', 'ln_b', 'proj_w', 'proj_b', 'convf_w', 'convf_b', 'convb_w',
                                         'convb_b', 'dbc_w', 'dtp_w', 'dtp_b', 'A_log', 'D_param')]
_OUTS = [((8, 256, 32, 32), 'float32')]


def kernel(**inputs):
    import numpy as _np
    import concourse.bacc as _bacc
    from concourse import mybir as _mybir
    from concourse.bass_utils import run_bass_kernel_spmd as _run

    nc = _bacc.Bacc("TRN2", target_bir_lowering=False, num_devices=1)
    arrays, args = {}, []
    for name in _INS:
        a = _np.ascontiguousarray(inputs[name])
        arrays[f"in_{name}_dram"] = a
        args.append(nc.dram_tensor(f"in_{name}_dram", a.shape, _mybir.dt.from_np(a.dtype), kind="ExternalInput").ap())
    for i, (shape, dtype) in enumerate(_OUTS):
        dt = _mybir.dt.from_np(_np.dtype(dtype))
        args.append(nc.dram_tensor(f"out_{i}_dram", shape, dt, kind="ExternalOutput").ap())
    conv_seq_kernel(nc, *args)
    r = _run(nc, [arrays], core_ids=[0])
    got = tuple(r.results[0][f"out_{i}_dram"] for i in range(len(_OUTS)))
    return got[0]
```
